# Optimizing a Trainium2 kernel written in Bass

```python
import numpy as np
import jax
import jax.numpy as jnp

def _softmax(x, axis=-1):
    return jax.nn.softmax(x, axis=axis)
def _gelu(x):
    return jax.nn.gelu(x, approximate=True)
def _silu(x):
    return jax.nn.silu(x)
def _sigmoid(x):
    return jax.nn.sigmoid(x)
def _layernorm(x, axis=-1, eps=1e-5):
    m = jnp.mean(x, axis=axis, keepdims=True)
    v = jnp.var(x, axis=axis, keepdims=True)
    return (x - m) / jnp.sqrt(v + eps)
def _scatter_add(tgt, idx, src, axis=0):
    return tgt.at[idx].add(src)
def _segment_sum(src, seg, n):
    return jax.ops.segment_sum(src, seg, n)

kernel_name = 'mk_conv_preact_d1_conv_nchw384_9683d1'

def setup_inputs(seed: int = 0):
    np.random.seed(seed)
    _w = jnp.asarray
    def _rec_inputs():
        import jax
        import jax.numpy as jnp
        _gk = jax.random.key(seed)
        x = -0.0002221 + 1 * jax.random.normal(jax.random.fold_in(_gk, 1), (16, 384, 64, 64), jnp.float32)
        return x
    x = _rec_inputs()
    def _L0_conv_setup():
        import jax, jax.numpy as jnp
        import numpy as np
        DIM = 384
        HEAD_DIM = 32
        NUM_HEADS = DIM // HEAD_DIM
        DOWN = 2
        EPS = 1e-12

        def conv1x1(x, w, b):
            y = jnp.einsum('oc,bchw->bohw', w, x)
            if b is not None:
                y = y + b[None, :, None, None]
            return y
        key = jax.random.key(seed)
        ks = jax.random.split(key, 7)
        s = 1.0 / np.sqrt(DIM)
        x = jax.random.normal(ks[0], (16, DIM, 64, 64), dtype=jnp.float32)
        qk_w = jax.random.normal(ks[1], (2 * DIM, DIM), dtype=jnp.float32) * s
        qk_b = jax.random.normal(ks[2], (2 * DIM,), dtype=jnp.float32) * 0.02
        v_w = jax.random.normal(ks[3], (DIM, DIM), dtype=jnp.float32) * s
        v_b = jax.random.normal(ks[4], (DIM,), dtype=jnp.float32) * 0.02
        proj_w = jax.random.normal(ks[5], (DIM, DIM), dtype=jnp.float32) * s
        proj_b = jax.random.normal(ks[6], (DIM,), dtype=jnp.float32) * 0.02
        temperature = jnp.ones((NUM_HEADS, 1, 1), dtype=jnp.float32)
        return {'x': x, 'qk_w': qk_w, 'qk_b': qk_b, 'v_w': v_w, 'v_b': v_b, 'proj_w': proj_w, 'proj_b': proj_b, 'temperature': temperature}
    _L0_conv_all = _L0_conv_setup()
    _L0_conv_in = {k: v for k, v in _L0_conv_all.items() if k in ('qk_w', 'qk_b', 'v_w', 'v_b', 'proj_w', 'proj_b', 'temperature', )}
    del _L0_conv_all

    return {
        "x": x,
        "L0_conv_qk_w": _L0_conv_in["qk_w"],
        "L0_conv_qk_b": _L0_conv_in["qk_b"],
        "L0_conv_v_w": _L0_conv_in["v_w"],
        "L0_conv_v_b": _L0_conv_in["v_b"],
        "L0_conv_proj_w": _L0_conv_in["proj_w"],
        "L0_conv_proj_b": _L0_conv_in["proj_b"],
        "L0_conv_temperature": _L0_conv_in["temperature"],
    }

def reference(x, L0_conv_qk_w, L0_conv_qk_b, L0_conv_v_w, L0_conv_v_b, L0_conv_proj_w, L0_conv_proj_b, L0_conv_temperature):
    import jax
    import jax.numpy as jnp
    def _L0_conv_ref(x, qk_w, qk_b, v_w, v_b, proj_w, proj_b, temperature):
        import jax, jax.numpy as jnp
        import numpy as np
        DIM = 384
        HEAD_DIM = 32
        NUM_HEADS = DIM // HEAD_DIM
        DOWN = 2
        EPS = 1e-12

        def conv1x1(x, w, b):
            y = jnp.einsum('oc,bchw->bohw', w, x)
            if b is not None:
                y = y + b[None, :, None, None]
            return y
        B, C, H, W = x.shape
        nh, hd = (NUM_HEADS, HEAD_DIM)
        v = conv1x1(x, v_w, v_b).reshape(B, nh, hd, H * W)
        Hd, Wd = (H // DOWN, W // DOWN)
        x_ = x.reshape(B, C, Hd, DOWN, Wd, DOWN).mean(axis=(3, 5))
        qk = conv1x1(x_, qk_w, qk_b).reshape(B, 2, nh, hd, Hd * Wd)
        q, k = (qk[:, 0], qk[:, 1])
        q = q / jnp.maximum(jnp.linalg.norm(q, axis=-1, keepdims=True), EPS)
        k = k / jnp.maximum(jnp.linalg.norm(k, axis=-1, keepdims=True), EPS)
        attn = jnp.einsum('bhdn,bhen->bhde', q, k) * temperature[None]
        attn = jax.nn.softmax(attn, axis=-1)
        out = jnp.einsum('bhde,bhen->bhdn', attn, v).reshape(B, C, H, W)
        return conv1x1(out, proj_w, proj_b)

    def _gn(v, G=32, eps=1e-5):
        B_, C_, H_, W_ = v.shape
        g = v.reshape(B_, G, C_ // G, H_, W_)
        m = jnp.mean(g, axis=(2, 3, 4), keepdims=True)
        s = jnp.var(g, axis=(2, 3, 4), keepdims=True)
        return ((g - m) / jnp.sqrt(s + eps)).reshape(v.shape)

    def _ln_c(v, eps=1e-6):
        m = jnp.mean(v, axis=1, keepdims=True)
        s = jnp.var(v, axis=1, keepdims=True)
        return (v - m) / jnp.sqrt(s + eps)

    def _ln_t(v, eps=1e-5):
        m = jnp.mean(v, axis=-1, keepdims=True)
        s = jnp.var(v, axis=-1, keepdims=True)
        return (v - m) / jnp.sqrt(s + eps)

    def _to_tokens(v):
        B_, C_, H_, W_ = v.shape
        return v.reshape(B_, C_, H_ * W_).transpose(0, 2, 1)
    def _from_tokens(t, like):
        B_, C_, H_, W_ = like.shape
        return t.transpose(0, 2, 1).reshape(B_, C_, H_, W_)

    x = x + _L0_conv_ref(_gn(x), L0_conv_qk_w, L0_conv_qk_b, L0_conv_v_w, L0_conv_v_b, L0_conv_proj_w, L0_conv_proj_b, L0_conv_temperature)
    return x


_drawn_inputs = setup_inputs


def setup_inputs(seed=0):
    import zlib

    import numpy as np

    out = dict(_drawn_inputs(seed))
    spreads = {'L0_conv_temperature': (1.0, 0.6)}
    factors = {'L0_conv_qk_w': 36.521, 'L0_conv_qk_b': 64.0, 'L0_conv_v_b': 22.959}
    for name, (base, spread) in spreads.items():
        noise = np.random.default_rng([zlib.crc32(name.encode()), seed]).standard_normal(out[name].shape)
        drawn = base * np.exp(spread * noise) if base else spread * noise
        out[name] = jnp.asarray(drawn.astype(out[name].dtype))
    for name, factor in factors.items():
        out[name] = (out[name] * factor).astype(out[name].dtype)
    return out
```

```python
from contextlib import ExitStack

import concourse.bass as bass
from concourse import mybir

F32 = mybir.dt.float32
F32R = mybir.dt.float32r
I32 = mybir.dt.int32
ALU = mybir.AluOpType
ACT = mybir.ActivationFunctionType
AX = mybir.AxisListType

P = 128
HEAD = 32
POOL = 2
GROUPS = 32
GN_EPS = 1e-5
NORM_EPS = 1e-12
MASKED = -1e30
RSQRT_MAGIC = float(0x5F3759DF)


def conv_attention_program(nc, x, qk_w, qk_b, v_w, v_b, proj_w, proj_b, temperature, out):
    B, C, H, W = x.shape
    NT = C // P
    HW = H * W
    CH = 512
    NCH = HW // CH
    NPOS = HW // (POOL * POOL)
    PCH = NPOS // NCH
    UNITS = NCH * NT
    GP = (C // GROUPS) // NT
    XSLOTS = 2 * NCH
    CG = C + 2
    KQ = 2 * P
    assert PCH == P and NT == 3 and C % GROUPS == 0 and B % 2 == 0 and NCH == 8

    xv = x.rearrange("b (p t) h w -> b p t (h w)", t=NT)
    ov = out.rearrange("b (p t) h w -> b p t (h w)", t=NT)

    POOL_AT = {8: 0, 10: 1, 12: 2, 14: 3, 16: 4, 18: 5, 21: 6, 23: 7}

    with ExitStack() as ctx:
        def sb(name, shape, dt=F32):
            return ctx.enter_context(nc.sbuf_tensor(name, shape, dt))

        def sem(name):
            return ctx.enter_context(nc.semaphore(name))

        xs = sb("xs", [P, XSLOTS, NT * CH])
        x_hi = sb("x_hi", [P, 2, NT, CH], F32R)
        x_lo = sb("x_lo", [P, 2, NT, CH], F32R)
        staged = sb("staged", [P, 2, NT, CH])
        wT_hi = sb("wT_hi", [P, NT, NT, KQ], F32R)
        wT_lo = sb("wT_lo", [P, NT, NT, KQ], F32R)
        wv_hi = sb("wv_hi", [P, NT, NT, P], F32R)
        wv_lo = sb("wv_lo", [P, NT, NT, P], F32R)
        wpT = sb("wpT", [P, NT, C])
        pooled = sb("pooled", [P, NT, NPOS])
        m_hi = sb("m_hi", [P, 2, NT, C], F32R)
        m_lo = sb("m_lo", [P, 2, NT, C], F32R)
        xT_hi = sb("xT_hi", [P, 2, CG], F32R)
        xT_lo = sb("xT_lo", [P, 2, CG], F32R)
        g_hi = sb("g_hi", [P, NT, CG], F32R)
        g_lo = sb("g_lo", [P, NT, CG], F32R)
        t_hi = sb("t_hi", [P, NT, KQ + 2], F32R)
        t_lo = sb("t_lo", [P, NT, KQ + 2], F32R)
        work = sb("work", [P, 3 * C])
        bq_row = sb("bq_row", [P, NT, P])
        ident = sb("ident", [P, P])
        own_head = sb("own_head", [P, P])
        group_avg = sb("group_avg", [P, P])
        bn = sb("bn", [P, NCH * NT, 6])
        bv_split = sb("bv_split", [P, NT, 2], F32R)
        small = sb("small", [P, 72])

        st = work[:, 0:C].rearrange("p (b e) -> p b e", b=NT)
        rows = work[:, C:2 * C].rearrange("p (b e) -> p b e", b=NT)
        logits = work[:, 2 * C:3 * C].rearrange("p (b e) -> p b e", b=NT)
        attn = work[:, 0:C].rearrange("p (b e) -> p b e", b=NT)
        m_full = work[:, :].rearrange("p (t o) -> p t o", t=NT)

        cursor = [0]

        def cols(n):
            a = cursor[0]
            cursor[0] += n
            return small[:, a:a + n]

        mv = cols(2)
        gmv = cols(2)
        dev = cols(1)
        dev2 = cols(1)
        var = cols(1)
        rstd = cols(1)
        negmean = cols(2)
        pool_scale = cols(1)
        pool_shift = cols(1)
        newton_a = cols(6)
        norm2 = cols(6)
        wsum = cols(6)
        norm_b = cols(6)
        rnorm = cols(6)
        rk_bk = cols(3)
        sum_q = cols(3)
        rq_temp = cols(3)
        neg_max = cols(3)
        exp_sum = cols(3)
        bias_raw = cols(3)
        kq_bias = small[:, 66:72].rearrange("p (s b) -> p s b", s=2)
        kq_bias_flat = small[:, 66:72]
        assert cursor[0] <= 66
        small2 = sb("small2", [P, 21])
        temp = small2[:, 0:3]
        bp = small2[:, 3:6]
        bv = small2[:, 6:9]
        bias = small2[:, 9:15]
        n_bias = small2[:, 15:21]

        main_bank = [ctx.enter_context(nc.psum_tensor(f"main{i}", [P, CH], F32)) for i in range(4)]
        bank_a, bank_b, bank_c, bank_d = [
            ctx.enter_context(nc.psum_tensor(f"chain{i}", [P, CH], F32)) for i in range(4)]

        raw_loaded = sem("raw_loaded")
        small_loaded = sem("small_loaded")
        x_loaded = [sem(f"x_loaded{s}") for s in range(XSLOTS)]
        out_stored = [sem(f"out_stored{s}") for s in range(2)]
        consts_step = sem("consts_step")
        consts_ready = sem("consts_ready")
        ones_ready = sem("ones_ready")
        w_transposed = sem("w_transposed")
        w_hi_ready = sem("w_hi_ready")
        w_lo_ready = sem("w_lo_ready")
        hi_ready = sem("hi_ready")
        lo_ready = sem("lo_ready")
        unit_done = sem("unit_done")
        evacuated = sem("evacuated")
        vec_step = sem("vec_step")
        act_step = sem("act_step")
        bn_taken = sem("bn_taken")
        pool_taken = sem("pool_taken")
        stats_ready = sem("stats_ready")
        gmean_done = sem("gmean_done")
        dev_ready = sem("dev_ready")
        gvar_done = sem("gvar_done")
        mean_ready = sem("mean_ready")
        pooled_ready = sem("pooled_ready")
        turned = sem("turned")
        xT_hi_ready = sem("xT_hi_ready")
        xT_lo_ready = sem("xT_lo_ready")
        gram_done = sem("gram_done")
        g_hi_ready = sem("g_hi_ready")
        g_lo_ready = sem("g_lo_ready")
        g_turned = sem("g_turned")
        g_hi_full = sem("g_hi_full")
        g_lo_full = sem("g_lo_full")
        sums_hi_ready = sem("sums_hi_ready")
        sums_lo_ready = sem("sums_lo_ready")
        t_done = sem("t_done")
        t_hi_ready = sem("t_hi_ready")
        t_lo_ready = sem("t_lo_ready")
        s_done = sem("s_done")
        s_read = sem("s_read")
        s_scaled = sem("s_scaled")
        s_turned = sem("s_turned")
        logits_ready = sem("logits_ready")
        exp_done = sem("exp_done")
        attn_ready = sem("attn_ready")
        p1_done = sem("p1_done")
        p1_hi_ready = sem("p1_hi_ready")
        p1_lo_ready = sem("p1_lo_ready")
        m_done = sem("m_done")
        m_scaled = sem("m_scaled")
        m_full_ready = sem("m_full_ready")
        m_hi_ready = sem("m_hi_ready")
        m_ready = sem("m_ready")
        bias_done = sem("bias_done")
        bias_ready = sem("bias_ready")

        def wait_count(eng, semaphore, value):
            if isinstance(value, int) and value <= 0:
                return
            eng.wait_ge(semaphore, value)

        class Step:

            def __init__(self, b, parity, half):
                self.b, self.parity, self.half = b, parity, half

        def fixed(b):
            return Step(b, b % 2, b // 2)

        def following(s, n):
            return Step(s.b + n, (s.parity + n) % 2, s.half + (s.parity + n) // 2)

        def pair(i):
            return Step(2 * i + 1, 1, i), Step(2 * i + 2, 0, i + 1)

        def slot(s, j):
            return NCH * s.parity + j

        raw = xs[:, XSLOTS - 3:XSLOTS, :].rearrange("p s n -> p (s n)")
        raw_qk = raw[:, 0:2 * NT * C].rearrange("p (k c) -> p k c", c=C)
        raw_v = raw[:, 2 * NT * C:3 * NT * C].rearrange("p (k c) -> p k c", c=C)
        raw_p = raw[:, 3 * NT * C:4 * NT * C].rearrange("p (t d) -> p t d", d=C)
        SMALL_LOADS = 4 + 2 + 1 + 1 + 1

        block = ctx.enter_context(nc.Block())

        @block.sync
        def _(sp):
            def load(s, j):
                sp.dma_start(xs[:, slot(s, j), :].rearrange("p (t n) -> p t n", t=NT),
                             xv[bass.ds(s.b, 1), :, :, j * CH:(j + 1) * CH].rearrange(
                                 "a p t n -> p (a t) n")).then_inc(x_loaded[slot(s, j)], 16)

            def store(s, j):
                sp.wait_ge(evacuated, UNITS * s.b + NT * (j + 1))
                sp.dma_start(ov[bass.ds(s.b, 1), :, :, j * CH:(j + 1) * CH].rearrange(
                    "a p t n -> p (a t) n"), staged[:, j % 2, :, :]).then_inc(out_stored[j % 2], 16)

            def reload(s, j):
                n = following(s, (j + 1) // NCH)
                sp.wait_ge(lo_ready, NCH * s.b + j + 2)
                load(following(n, 2), (j + 1) % NCH)

            def step(s, reloads):
                for j in range(NCH):
                    if j < reloads:
                        reload(s, j)
                    store(s, j)

            sp.dma_start(raw_qk, qk_w.rearrange("(k p) c -> p k c", p=P)).then_inc(raw_loaded, 16)
            sp.dma_start(raw_v, v_w.rearrange("(k p) c -> p k c", p=P)).then_inc(raw_loaded, 16)
            sp.dma_start(raw_p, proj_w.rearrange("(p t) d -> p t d", t=NT)).then_inc(raw_loaded, 16)
            for j in range(NCH):
                load(fixed(0), j)
            with nc.allow_non_contiguous_dma(reason="a few hundred single words, once"):
                for hh in range(4):
                    sp.dma_start(temp[HEAD * hh:HEAD * (hh + 1), :],
                                 temperature.rearrange("(b h) x y -> h (b x y)", h=4)[hh:hh + 1, :]
                                 .to_broadcast([HEAD, NT])).then_inc(small_loaded, 16)
                for k in range(2):
                    sp.dma_start(kq_bias[:, 1 - k, :], qk_b[k * C:(k + 1) * C].rearrange("(b p) -> p b", p=P))\
                        .then_inc(small_loaded, 16)
                sp.dma_start(bv, v_b.rearrange("(b p) -> p b", p=P)).then_inc(small_loaded, 16)
                sp.dma_start(bp, proj_b.rearrange("(p t) -> p t", t=NT)).then_inc(small_loaded, 16)
                sp.dma_start(bq_row[:, :, :].rearrange("p b e -> p (b e)"),
                             qk_b[0:C].rearrange("(a n) -> a n", a=1).to_broadcast([P, C])).then_inc(small_loaded, 16)
            for j in range(NCH - 3):
                load(fixed(1), j)
            sp.wait_ge(w_lo_ready, NT * NT + NT)
            sp.wait_ge(w_hi_ready, NT * NT + 2 * NT)
            for j in range(NCH - 3, NCH):
                load(fixed(1), j)
            sp.wait_ge(lo_ready, 1)
            load(fixed(2), 0)
            step(fixed(0), NCH)
            with sp.Fori(0, (B - 4) // 2) as i:
                for s in pair(i):
                    step(s, NCH)
            step(fixed(B - 3), NCH - 1)
            step(fixed(B - 2), 0)
            step(fixed(B - 1), 0)
            for s in range(2):
                sp.wait_ge(out_stored[s], 16 * B * NCH // 2)

        @block.gpsimd
        def _(pool):
            nc.gpsimd.memset(ident[:, :], 0.0).then_inc(consts_step, 1)
            nc.gpsimd.memset(own_head[:, :], 0.0).then_inc(consts_step, 1)
            nc.gpsimd.memset(group_avg[:, :], 1.0 / GP).then_inc(consts_step, 1)
            pool.wait_ge(consts_step, 3)
            nc.gpsimd.affine_select(out=ident[:, :], in_=ident[:, :], compare_op=ALU.not_equal, fill=1.0,
                                    base=0, pattern=[[-1, P]], channel_multiplier=1).then_inc(consts_ready, 1)
            for m, width, fill in ((own_head, HEAD, MASKED), (group_avg, GP, 0.0)):
                v = m[:, :].rearrange("p (k w) -> p k w", w=width)
                nc.gpsimd.affine_select(out=v, in_=v, compare_op=ALU.is_ge, fill=fill, base=0,
                                        pattern=[[-width, P // width], [0, width]],
                                        channel_multiplier=1).then_inc(consts_step, 1)
            pool.wait_ge(consts_step, 5)
            for m, width, fill in ((own_head, HEAD, MASKED), (group_avg, GP, 0.0)):
                v = m[:, :].rearrange("p (k w) -> p k w", w=width)
                nc.gpsimd.affine_select(out=v, in_=v, compare_op=ALU.is_ge, fill=fill, base=width - 1,
                                        pattern=[[width, P // width], [0, width]],
                                        channel_multiplier=-1).then_inc(consts_ready, 1)

        @block.tensor
        def _(pe):
            def three_passes(dst, lhs, rhs, start, stop, skip=False):
                nc.tensor.matmul(dst, lhs[0], rhs[0], start=start, stop=False, skip_group_check=skip)
                nc.tensor.matmul(dst, lhs[0], rhs[1], start=False, stop=False, skip_group_check=skip)
                return nc.tensor.matmul(dst, lhs[1], rhs[0], start=False, stop=stop, skip_group_check=skip)

            def unit(s, u):
                j, o = divmod(u, NT)
                if u == 0:
                    pe.wait_ge(m_ready, s.b + 1)
                if o == 0:
                    pe.wait_ge(lo_ready, NCH * s.b + j + 1)
                wait_count(pe, evacuated, UNITS * s.b + u - 3)
                for t in range(NT):
                    last = three_passes(
                        main_bank[u % 4][:, :],
                        (m_hi[:, s.parity, t, o * P:(o + 1) * P], m_lo[:, s.parity, t, o * P:(o + 1) * P]),
                        (x_hi[:, j % 2, t, :], x_lo[:, j % 2, t, :]), t == 0, t == NT - 1)
                last.then_inc(unit_done, 1)

            def group_mean(s):
                pe.wait_ge(stats_ready, s.b + 1)
                wait_count(pe, m_scaled, s.b)
                wait_count(pe, bias_ready, s.b)
                nc.tensor.matmul(bank_c[:, 0:2], group_avg[:, :], mv, start=True, stop=True)\
                    .then_inc(gmean_done, 1)

            def group_var(s):
                pe.wait_ge(dev_ready, s.b + 1)
                nc.tensor.matmul(bank_d[:, 0:1], group_avg[:, :], dev2, start=True, stop=True)\
                    .then_inc(gvar_done, 1)

            def turn(s, c):
                bank = bank_c if c % 2 == 0 else bank_d
                if c % (NCH // 2) == 0:
                    pe.wait_ge(pooled_ready, 2 * s.b + c // (NCH // 2) + 1)
                if c >= 2:
                    pe.wait_ge(xT_hi_ready, NCH * s.b + c - 1)
                    pe.wait_ge(xT_lo_ready, NCH * s.b + c - 1)
                for t in range(NT):
                    last = nc.tensor.transpose(bank[:, t * P:(t + 1) * P],
                                               pooled[:, t, c * PCH:(c + 1) * PCH], ident[:, :])
                last.then_inc(turned, 1)

            def gram(s, c):
                pe.wait_ge(xT_hi_ready, NCH * s.b + c + 1)
                pe.wait_ge(xT_lo_ready, NCH * s.b + c + 1)
                h, l = xT_hi[:, c % 2, :], xT_lo[:, c % 2, :]
                first, final = c == 0, c == NCH - 1
                three_passes(bank_a[:, 0:CG], (h[:, 0:P], l[:, 0:P]), (h[:, 0:CG], l[:, 0:CG]), first, final)
                three_passes(bank_b[:, 0:CG - P], (h[:, P:2 * P], l[:, P:2 * P]),
                             (h[:, P:CG], l[:, P:CG]), first, final, skip=True)
                three_passes(bank_b[:, CG - P:2 * CG - 3 * P], (h[:, 2 * P:3 * P], l[:, 2 * P:3 * P]),
                             (h[:, 2 * P:CG], l[:, 2 * P:CG]), False, final, skip=True)\
                    .then_inc(gram_done, 1)

            def turn_gram(s):
                for ready, g, bank in ((g_hi_ready, g_hi, bank_c), (g_lo_ready, g_lo, bank_d)):
                    pe.wait_ge(ready, s.b + 1)
                    if bank is bank_c:
                        pe.wait_ge(xT_hi_ready, NCH * (s.b + 1))
                        pe.wait_ge(xT_lo_ready, NCH * (s.b + 1))
                    for n, (row, col) in enumerate(((0, 1), (0, 2), (1, 2))):
                        last = nc.tensor.transpose(bank[:, n * P:(n + 1) * P],
                                                   g[:, row, col * P:(col + 1) * P].bitcast(F32), ident[:, :])
                    last.then_inc(g_turned, 1)

            def t_block(s, blk):
                if blk == 0:
                    pe.wait_ge(g_hi_full, s.b + 1)
                    pe.wait_ge(g_lo_full, s.b + 1)
                else:
                    pe.wait_ge(t_hi_ready, NT * s.b + blk)
                    pe.wait_ge(t_lo_ready, NT * s.b + blk)
                for i, dst in enumerate((bank_a[:, 0:KQ], bank_a[:, KQ:2 * KQ], bank_b[:, 0:KQ])):
                    for k in range(NT):
                        last = three_passes(dst, (g_hi[:, k, i * P:(i + 1) * P], g_lo[:, k, i * P:(i + 1) * P]),
                                            (wT_hi[:, k, blk, :], wT_lo[:, k, blk, :]), k == 0, k == NT - 1)
                last.then_inc(t_done, 1)

            def s_block(s, blk):
                pe.wait_ge(t_hi_ready, NT * s.b + blk + 1)
                pe.wait_ge(t_lo_ready, NT * s.b + blk + 1)
                if blk == 0:
                    pe.wait_ge(sums_hi_ready, s.b + 1)
                    pe.wait_ge(sums_lo_ready, s.b + 1)
                if blk == 2:
                    pe.wait_ge(s_read, NT * s.b + 1)
                bank = bank_d if blk == 1 else bank_c
                for w0, dst, c0 in ((0, bank[:, 0:KQ + 2], 0), (P, bank[:, KQ + 2:KQ + 2 + P + 2], P)):
                    for k in range(NT):
                        last = three_passes(dst, (wT_hi[:, k, blk, w0:w0 + P], wT_lo[:, k, blk, w0:w0 + P]),
                                            (t_hi[:, k, c0:KQ + 2], t_lo[:, k, c0:KQ + 2]), k == 0, k == NT - 1)
                last.then_inc(s_done, 1)

            def turn_scores(s):
                pe.wait_ge(s_scaled, s.b + 1)
                for src, bank in ((st, bank_c), (rows, bank_d)):
                    for blk in range(NT):
                        last = nc.tensor.transpose(bank[:, blk * P:(blk + 1) * P], src[:, blk, :], ident[:, :])
                last.then_inc(s_turned, 1)

            def fold_proj(s):
                pe.wait_ge(attn_ready, s.b + 1)
                for blk, bank in enumerate((bank_a, bank_b, bank_d)):
                    last = nc.tensor.matmul(bank[:, 0:C], attn[:, blk, :], wpT[:, blk, :], start=True, stop=True)
                last.then_inc(p1_done, 1)

            def fold_value(s):
                pe.wait_ge(p1_hi_ready, s.b + 1)
                pe.wait_ge(p1_lo_ready, s.b + 1)
                for t, bank in enumerate((bank_c, bank_a, bank_b)):
                    for blk in range(NT):
                        last = three_passes(bank[:, 0:C], (wv_hi[:, blk, t, :], wv_lo[:, blk, t, :]),
                                            (g_hi[:, blk, 0:C], g_lo[:, blk, 0:C]), blk == 0, blk == NT - 1)
                last.then_inc(m_done, 1)
                for o in range(NT):
                    for blk in range(NT):
                        for part, g in enumerate((g_hi, g_lo)):
                            last = nc.tensor.matmul(bank_d[:, 2 * o:2 * o + 2], g[:, blk, o * P:(o + 1) * P],
                                                    bv_split[:, blk, :], start=(blk == 0 and part == 0),
                                                    stop=(blk == NT - 1 and part == 1))
                last.then_inc(bias_done, 1)

            def chain(s, u):
                if u == 1:
                    group_mean(s)
                if u == 2:
                    group_var(s)
                if 5 <= u <= 8:
                    gram(s, 2 * (u - 5))
                    gram(s, 2 * (u - 5) + 1)
                if 4 <= u <= 7:
                    turn(s, 2 * (u - 4))
                    turn(s, 2 * (u - 4) + 1)
                if u == 9:
                    turn_gram(s)
                if 11 <= u <= 13:
                    s_block(s, u - 11)
                if 10 <= u <= 12:
                    t_block(s, u - 10)
                if u == 16:
                    turn_scores(s)
                if u == 18:
                    fold_proj(s)
                if u == 20:
                    fold_value(s)

            pe.wait_ge(consts_ready, 3)
            pe.wait_ge(raw_loaded, 16 * 3)
            n = 0
            for blk in range(NT):
                for t in range(NT):
                    bank = main_bank[n % 4]
                    if n >= 4:
                        pe.wait_ge(w_hi_ready, n - 3)
                        pe.wait_ge(w_lo_ready, n - 3)
                    for half, row in ((0, NT + blk), (1, blk)):
                        last = nc.tensor.transpose(bank[:, half * P:(half + 1) * P],
                                                   raw_qk[:, row, :].rearrange("p (c t) -> p t c", t=NT)[:, t, :],
                                                   ident[:, :])
                    last.then_inc(w_transposed, 1)
                    n += 1
            for blk in range(NT):
                bank = (bank_a, bank_b, bank_c)[blk]
                for t in range(NT):
                    last = nc.tensor.transpose(bank[:, t * P:(t + 1) * P],
                                               raw_p[:, t, blk * P:(blk + 1) * P], ident[:, :])
                last.then_inc(w_transposed, 1)
            pe.wait_ge(w_hi_ready, NT * NT + 2 * NT)
            pe.wait_ge(w_lo_ready, NT * NT + NT)
            pe.wait_ge(ones_ready, 2)
            for u in range(UNITS):
                chain(fixed(0), u)

            def step(s, with_chain=True):
                for u in range(UNITS):
                    if with_chain:
                        chain(following(s, 1), u)
                    unit(s, u)

            step(fixed(0))
            with pe.Fori(0, (B - 2) // 2) as i:
                for s in pair(i):
                    step(s)
            step(fixed(B - 1), with_chain=False)

        @block.scalar
        def _(act):
            def split_hi(s, j):
                act.wait_ge(x_loaded[slot(s, j)], 16 * (s.half + 1))
                if j < 2:
                    act.wait_ge(mean_ready, s.b + 1)
                wait_count(act, unit_done, UNITS * s.b + NT * (j - 1))
                nc.scalar.activation(x_hi[:, j % 2, :, :].rearrange("p t n -> p (t n)"), xs[:, slot(s, j), :],
                                     ACT.Identity, bias=negmean[:, s.parity:s.parity + 1]).then_inc(hi_ready, 1)

            def evacuate(s, u):
                j, o = divmod(u, NT)
                if u == 0:
                    act.wait_ge(bias_ready, s.b + 1)
                if o == 0:
                    wait_count(act, out_stored[j % 2], 16 * ((NCH // 2) * s.b + j // 2))
                act.wait_ge(unit_done, UNITS * s.b + u + 1)
                nc.scalar.activation(staged[:, j % 2, o, :], main_bank[u % 4][:, :], ACT.Identity,
                                     bias=bias[:, NT * s.parity + o:NT * s.parity + o + 1]).then_inc(evacuated, 1)

            def xT_high(s, c):
                act.wait_ge(turned, NCH * s.b + c + 1)
                if c >= 2:
                    act.wait_ge(gram_done, NCH * s.b + c - 1)
                bank = bank_c if c % 2 == 0 else bank_d
                nc.scalar.activation(xT_hi[:, c % 2, 0:C], bank[:, 0:C], ACT.Copy).then_inc(xT_hi_ready, 1)

            def gram_high(s):
                act.wait_ge(gram_done, NCH * (s.b + 1))
                nc.scalar.activation(g_hi[:, 0, :], bank_a[:, 0:CG], ACT.Copy)
                nc.scalar.activation(g_hi[:, 1, P:CG], bank_b[:, 0:CG - P], ACT.Copy)
                nc.scalar.activation(g_hi[:, 2, 2 * P:CG], bank_b[:, CG - P:2 * CG - 3 * P], ACT.Copy)\
                    .then_inc(g_hi_ready, 1)

            def gram_high_lower(s):
                act.wait_ge(g_turned, 2 * s.b + 1)
                nc.scalar.activation(g_hi[:, 1, 0:P], bank_c[:, 0:P], ACT.Copy)
                nc.scalar.activation(g_hi[:, 2, 0:2 * P], bank_c[:, P:3 * P], ACT.Copy).then_inc(g_hi_full, 1)
                act.wait_ge(g_hi_ready, s.b + 1)
                wait_count(act, s_done, NT * s.b)
                nc.scalar.activation(t_hi[:, :, KQ:KQ + 2], g_hi[:, :, C:CG].bitcast(F32), ACT.Copy)\
                    .then_inc(sums_hi_ready, 1)

            def t_high(s, blk):
                act.wait_ge(t_done, NT * s.b + blk + 1)
                if blk == 0:
                    wait_count(act, s_done, NT * s.b)
                nc.scalar.activation(t_hi[:, 0:2, 0:KQ], bank_a[:, :].rearrange("p (i c) -> p i c", i=2), ACT.Copy)
                nc.scalar.activation(t_hi[:, 2, 0:KQ], bank_b[:, 0:KQ], ACT.Copy).then_inc(t_hi_ready, 1)

            def exps(s):
                act.wait_ge(logits_ready, s.b + 1)
                for blk in range(NT):
                    last = nc.scalar.activation(attn[:, blk, :], logits[:, blk, :], ACT.Exp,
                                                bias=neg_max[:, blk:blk + 1], accum_out=exp_sum[:, blk:blk + 1])
                last.then_inc(exp_done, 1)

            def p1_high(s):
                act.wait_ge(p1_done, s.b + 1)
                for blk, bank in enumerate((bank_a, bank_b, bank_d)):
                    last = nc.scalar.activation(g_hi[:, blk, 0:C], bank[:, 0:C], ACT.Copy)
                last.then_inc(p1_hi_ready, 1)

            def scale_m(s):
                act.wait_ge(m_done, s.b + 1)
                for t, bank in enumerate((bank_c, bank_a, bank_b)):
                    last = nc.scalar.activation(m_full[:, t, :], bank[:, 0:C], ACT.Copy, scale=rstd)
                last.then_inc(m_scaled, 1)

            def m_high(s):
                act.wait_ge(m_full_ready, s.b + 1)
                nc.scalar.activation(m_hi[:, s.parity, :, :].rearrange("p t o -> p (t o)"), work[:, :], ACT.Copy)\
                    .then_inc(m_hi_ready, 1)

            def chain(s, u):
                if 4 <= u <= 7:
                    xT_high(s, 2 * (u - 4))
                    xT_high(s, 2 * (u - 4) + 1)
                if u == 8:
                    gram_high(s)
                if u == 9:
                    gram_high_lower(s)
                if 10 <= u <= 12:
                    t_high(s, u - 10)
                if u == 17:
                    exps(s)
                if u == 18:
                    p1_high(s)
                if u == 21:
                    scale_m(s)
                    m_high(s)

            for n in range(NT * NT):
                blk, t = divmod(n, NT)
                act.wait_ge(w_transposed, n + 1)
                nc.scalar.activation(wT_hi[:, t, blk, :], main_bank[n % 4][:, 0:KQ], ACT.Copy)\
                    .then_inc(w_hi_ready, 1)
            for blk, bank in enumerate((bank_a, bank_b, bank_c)):
                act.wait_ge(w_transposed, NT * NT + blk + 1)
                nc.scalar.activation(wpT[:, blk, :], bank[:, 0:C], ACT.Copy).then_inc(w_hi_ready, 1)
            for blk in range(NT):
                nc.scalar.activation(wv_hi[:, blk, :, :], raw_v[:, blk, :].rearrange("p (c t) -> p t c", t=NT),
                                     ACT.Copy).then_inc(w_hi_ready, 1)
            act.wait_ge(small_loaded, 16 * SMALL_LOADS)
            nc.scalar.activation(bv_split[:, :, 0], bv, ACT.Copy).then_inc(w_hi_ready, 1)

            for u in range(UNITS):
                chain(fixed(0), u)
            split_hi(fixed(0), 0)
            split_hi(fixed(0), 1)

            def step(s, with_chain=True):
                for u in range(UNITS):
                    if with_chain:
                        chain(following(s, 1), u)
                    evacuate(s, u)
                    j, o = divmod(u, NT)
                    if o == NT - 1:
                        if j + 2 < NCH:
                            split_hi(s, j + 2)
                        elif with_chain:
                            split_hi(following(s, 1), j + 2 - NCH)

            step(fixed(0))
            with act.Fori(0, (B - 2) // 2) as i:
                for s in pair(i):
                    step(s)
            step(fixed(B - 1), with_chain=False)

        @block.vector
        def _(dve):
            links = {"base": 0, "count": 0, "setup": 0, "per_image": None}

            def link(ins):
                links["count"] += 1
                ins.then_inc(vec_step, 1)
                dve.wait_ge(vec_step, links["base"] + links["count"])

            def open_links(s):
                links["count"] = 0
                links["base"] = links["setup"] + (0 if links["per_image"] is None else links["per_image"] * s.b)

            def close_links():
                assert links["per_image"] in (None, links["count"])
                links["per_image"] = links["count"]

            def rsqrt(y, v):
                a = newton_a[:, 0:v.shape[1]]
                link(nc.vector.tensor_scalar(a.bitcast(I32), v.bitcast(I32), 1, None, ALU.logical_shift_right))
                link(nc.vector.tensor_scalar(y.bitcast(I32), a.bitcast(I32), -1.0, RSQRT_MAGIC, ALU.mult, ALU.add))
                for _ in range(3):
                    link(nc.vector.scalar_tensor_tensor(out=a, in0=y, scalar=-0.5, in1=v,
                                                        op0=ALU.mult, op1=ALU.mult))
                    link(nc.vector.tensor_tensor(a, a, y, ALU.mult))
                    link(nc.vector.scalar_tensor_tensor(out=y, in0=a, scalar=1.5, in1=y,
                                                        op0=ALU.add, op1=ALU.mult))

            def split_lo(s, j):
                dve.wait_ge(hi_ready, NCH * s.b + j + 1)
                nc.vector.scalar_tensor_tensor(
                    out=x_lo[:, j % 2, :, :].rearrange("p t n -> p (t n)"), in0=xs[:, slot(s, j), :],
                    scalar=negmean[:, s.parity:s.parity + 1],
                    in1=x_hi[:, j % 2, :, :].rearrange("p t n -> p (t n)").bitcast(F32),
                    op0=ALU.add, op1=ALU.subtract).then_inc(lo_ready, 1)

            def take_stats(s, j):
                dve.wait_ge(x_loaded[slot(s, j)], 16 * (s.half + 1))
                for t in range(NT):
                    nc.vector.bn_stats(bn[:, NT * j + t, :], xs[:, slot(s, j), t * CH:(t + 1) * CH])\
                        .then_inc(bn_taken, 1)

            def take_pool(s, j):
                if j == 0:
                    dve.wait_ge(x_loaded[slot(s, j)], 16 * (s.half + 1))
                    wait_count(dve, turned, NCH * s.b)
                else:
                    dve.wait_ge(x_loaded[slot(s, j)], 16 * (s.half + 1))
                rows_in = xs[:, slot(s, j), :].rearrange("p (r a c w) -> p r c a w", a=POOL, w=POOL, c=W // POOL)
                dst = pooled[:, :, j * PCH:(j + 1) * PCH]
                nc.vector.tensor_reduce(dst, rows_in, AX.XY, ALU.add).then_inc(pool_taken, 1)

            def group_stats(s):
                dve.wait_ge(bn_taken, NT * NCH * (s.b + 1))
                nc.vector.memset(dev, 0.0)
                nc.vector.bn_aggr(mv, bn[:, :, :].rearrange("p k s -> p (k s)")).then_inc(stats_ready, 1)

            def group_dev(s):
                dve.wait_ge(gmean_done, s.b + 1)
                dve.wait_ge(stats_ready, s.b + 1)
                link(nc.vector.tensor_copy(gmv, bank_c[:, 0:2]))
                link(nc.vector.tensor_tensor(dev, mv[:, 0:1], gmv[:, 0:1], ALU.subtract))
                nc.vector.tensor_tensor(dev2, dev, dev, ALU.mult).then_inc(dev_ready, 1)

            def group_scale(s):
                dve.wait_ge(gvar_done, s.b + 1)
                link(nc.vector.scalar_tensor_tensor(out=var, in0=bank_d[:, 0:1], scalar=GN_EPS, in1=gmv[:, 1:2],
                                                    op0=ALU.add, op1=ALU.add))
                rsqrt(rstd, var)
                nm = negmean[:, s.parity:s.parity + 1]
                link(nc.vector.tensor_scalar(nm, gmv[:, 0:1], -1.0, None, ALU.mult))
                link(nc.vector.tensor_scalar(pool_scale, rstd, 1.0 / (POOL * POOL), None, ALU.mult))
                nc.vector.tensor_tensor(pool_shift, nm, rstd, ALU.mult).then_inc(mean_ready, 1)
                dve.wait_ge(mean_ready, s.b + 1)
                dve.wait_ge(pool_taken, NCH * (s.b + 1))
                for half in range(2):
                    v = pooled[:, :, half * NPOS // 2:(half + 1) * NPOS // 2]
                    nc.vector.tensor_scalar(v, v, pool_scale, pool_shift, ALU.mult, ALU.add)\
                        .then_inc(pooled_ready, 1)

            def xT_low(s, c):
                dve.wait_ge(xT_hi_ready, NCH * s.b + c + 1)
                bank = bank_c if c % 2 == 0 else bank_d
                nc.vector.tensor_tensor(xT_lo[:, c % 2, 0:C], bank[:, 0:C], xT_hi[:, c % 2, 0:C].bitcast(F32),
                                        ALU.subtract).then_inc(xT_lo_ready, 1)

            def gram_low(s):
                dve.wait_ge(g_hi_ready, s.b + 1)
                for i, src in ((0, bank_a[:, 0:CG]), (1, bank_b[:, 0:CG - P]), (2, bank_b[:, CG - P:2 * CG - 3 * P])):
                    last = nc.vector.tensor_tensor(g_lo[:, i, i * P:CG], src, g_hi[:, i, i * P:CG].bitcast(F32),
                                                   ALU.subtract)
                last.then_inc(g_lo_ready, 1)

            def gram_low_lower(s):
                dve.wait_ge(g_turned, 2 * s.b + 2)
                nc.vector.tensor_copy(g_lo[:, 1, 0:P], bank_d[:, 0:P])
                nc.vector.tensor_copy(g_lo[:, 2, 0:2 * P], bank_d[:, P:3 * P]).then_inc(g_lo_full, 1)
                dve.wait_ge(g_lo_ready, s.b + 1)
                wait_count(dve, s_done, NT * s.b)
                nc.vector.tensor_copy(t_lo[:, :, KQ:KQ + 2], g_lo[:, :, C:CG]).then_inc(sums_lo_ready, 1)

            def t_low(s, blk):
                dve.wait_ge(t_hi_ready, NT * s.b + blk + 1)
                nc.vector.tensor_tensor(t_lo[:, 0:2, 0:KQ], bank_a[:, :].rearrange("p (i c) -> p i c", i=2),
                                        t_hi[:, 0:2, 0:KQ].bitcast(F32), ALU.subtract)
                nc.vector.tensor_tensor(t_lo[:, 2, 0:KQ], bank_b[:, 0:KQ], t_hi[:, 2, 0:KQ].bitcast(F32),
                                        ALU.subtract).then_inc(t_lo_ready, 1)

            def read_scores(s, blk):
                dve.wait_ge(s_done, NT * s.b + blk + 1)
                if blk == 0:
                    wait_count(dve, m_hi_ready, s.b)
                bank = bank_d if blk == 1 else bank_c
                link(nc.vector.tensor_copy(wsum.rearrange("p (s b) -> p s b", s=2)[:, :, blk],
                                           bank[:, KQ:KQ + P + 3:P + 2]))
                nc.vector.scalar_tensor_tensor(out=st[:, blk, :], in0=bq_row[:, blk, :], scalar=wsum[:, blk:blk + 1],
                                               in1=bank[:, P:2 * P], op0=ALU.mult, op1=ALU.add)
                nc.vector.scalar_tensor_tensor(out=rows[:, blk, :], in0=bank[:, 0:P], scalar=1.0, in1=ident[:, :],
                                               op0=ALU.mult, op1=ALU.mult, accum_out=norm2[:, blk:blk + 1])
                nc.vector.scalar_tensor_tensor(out=logits[:, blk, :], in0=bank[:, KQ + 2:KQ + 2 + P], scalar=1.0,
                                               in1=ident[:, :], op0=ALU.mult, op1=ALU.mult,
                                               accum_out=norm2[:, NT + blk:NT + blk + 1]).then_inc(s_read, 1)

            def scale_scores(s):
                dve.wait_ge(s_read, NT * (s.b + 1))
                link(nc.vector.scalar_tensor_tensor(out=norm_b, in0=wsum, scalar=2.0, in1=n_bias,
                                                    op0=ALU.mult, op1=ALU.add))
                link(nc.vector.tensor_tensor(norm_b, norm_b, kq_bias_flat, ALU.mult))
                link(nc.vector.tensor_tensor(norm_b, norm_b, norm2, ALU.add))
                link(nc.vector.tensor_scalar(norm_b, norm_b, NORM_EPS * NORM_EPS, None, ALU.max))
                rsqrt(rnorm, norm_b)
                link(nc.vector.tensor_tensor(rk_bk, rnorm[:, 0:NT], kq_bias_flat[:, 0:NT], ALU.mult))
                nc.vector.tensor_tensor(st, st, rnorm[:, 0:NT].unsqueeze(2).to_broadcast([P, NT, P]), ALU.mult)
                nc.vector.tensor_copy(rows, rk_bk.unsqueeze(2).to_broadcast([P, NT, P])).then_inc(s_scaled, 1)
                link(nc.vector.tensor_tensor(sum_q, wsum[:, NT:2 * NT], n_bias[:, NT:2 * NT], ALU.add))
                link(nc.vector.tensor_tensor(rq_temp, rnorm[:, NT:2 * NT], temp, ALU.mult))

            def make_logits(s):
                dve.wait_ge(s_turned, s.b + 1)
                v = [bank[:, 0:C].rearrange("p (b e) -> p b e", b=NT) for bank in (bank_c, bank_d)]
                link(nc.vector.tensor_tensor(rows, v[1], sum_q.unsqueeze(2).to_broadcast([P, NT, P]), ALU.mult))
                link(nc.vector.tensor_tensor(rows, v[0], rows, ALU.add))
                for blk in range(NT):
                    last = nc.vector.scalar_tensor_tensor(out=logits[:, blk, :], in0=rows[:, blk, :],
                                                          scalar=rq_temp[:, blk:blk + 1], in1=own_head[:, :],
                                                          op0=ALU.mult, op1=ALU.add)
                link(last)
                nc.vector.tensor_reduce(neg_max, logits, AX.X, ALU.max, negate=True).then_inc(logits_ready, 1)

            def normalise_attn(s):
                dve.wait_ge(exp_done, s.b + 1)
                link(nc.vector.reciprocal(exp_sum, exp_sum))
                nc.vector.tensor_tensor(attn, attn, exp_sum.unsqueeze(2).to_broadcast([P, NT, P]), ALU.mult)\
                    .then_inc(attn_ready, 1)

            def p1_low(s):
                dve.wait_ge(p1_hi_ready, s.b + 1)
                for blk, bank in enumerate((bank_a, bank_b, bank_d)):
                    last = nc.vector.tensor_tensor(g_lo[:, blk, 0:C], bank[:, 0:C], g_hi[:, blk, 0:C].bitcast(F32),
                                                   ALU.subtract)
                last.then_inc(p1_lo_ready, 1)

            def add_identity(s):
                dve.wait_ge(m_scaled, s.b + 1)
                for t in range(NT):
                    d = m_full[:, t, t * P:(t + 1) * P]
                    last = nc.vector.tensor_tensor(d, d, ident[:, :], ALU.add)
                last.then_inc(m_full_ready, 1)

            def m_low(s):
                dve.wait_ge(m_hi_ready, s.b + 1)
                nc.vector.tensor_tensor(m_lo[:, s.parity, :, :].rearrange("p t o -> p (t o)"), work[:, :],
                                        m_hi[:, s.parity, :, :].rearrange("p t o -> p (t o)").bitcast(F32),
                                        ALU.subtract).then_inc(m_ready, 1)

            def make_bias(s):
                dve.wait_ge(bias_done, s.b + 1)
                link(nc.vector.tensor_reduce(bias_raw, bank_d[:, 0:2 * NT].rearrange("p (o h) -> p o h", h=2),
                                             AX.X, ALU.add))
                nc.vector.scalar_tensor_tensor(out=bias[:, NT * s.parity:NT * (s.parity + 1)], in0=bias_raw,
                                               scalar=gmv[:, 0:1], in1=bp, op0=ALU.add, op1=ALU.add)\
                    .then_inc(bias_ready, 1)

            def chain(s, u):
                if u == 0:
                    open_links(s)
                    group_stats(s)
                if u == 1:
                    group_dev(s)
                if u == 2:
                    group_scale(s)
                if 4 <= u <= 7:
                    xT_low(s, 2 * (u - 4))
                    xT_low(s, 2 * (u - 4) + 1)
                if u == 8:
                    gram_low(s)
                if u == 9:
                    gram_low_lower(s)
                if 10 <= u <= 12:
                    t_low(s, u - 10)
                if 11 <= u <= 13:
                    read_scores(s, u - 11)
                if u == 14:
                    scale_scores(s)
                if u == 16:
                    make_logits(s)
                if u == 17:
                    normalise_attn(s)
                if u == 18:
                    p1_low(s)
                if u == 21:
                    add_identity(s)
                    m_low(s)
                if u == 22:
                    make_bias(s)
                    close_links()

            one = small[:, 0:2]
            link(nc.vector.memset(one, 1.0))
            for c in range(2):
                nc.vector.tensor_copy(xT_hi[:, c, C:CG], one)
            nc.vector.tensor_scalar(xT_lo[:, 0, C:CG], one, 0.0, None, ALU.mult).then_inc(ones_ready, 1)
            nc.vector.tensor_scalar(xT_lo[:, 1, C:CG], one, 0.0, None, ALU.mult).then_inc(ones_ready, 1)
            dve.wait_ge(ones_ready, 2)
            dve.wait_ge(small_loaded, 16 * SMALL_LOADS)
            link(nc.vector.tensor_scalar(n_bias, kq_bias_flat, float(NPOS), None, ALU.mult))
            for n in range(NT * NT):
                blk, t = divmod(n, NT)
                dve.wait_ge(w_hi_ready, n + 1)
                nc.vector.tensor_tensor(wT_lo[:, t, blk, :], main_bank[n % 4][:, 0:KQ],
                                        wT_hi[:, t, blk, :].bitcast(F32), ALU.subtract).then_inc(w_lo_ready, 1)
            for blk in range(NT):
                dve.wait_ge(w_hi_ready, NT * NT + NT + blk + 1)
                nc.vector.tensor_tensor(wv_lo[:, blk, :, :], raw_v[:, blk, :].rearrange("p (c t) -> p t c", t=NT),
                                        wv_hi[:, blk, :, :].bitcast(F32), ALU.subtract).then_inc(w_lo_ready, 1)
            dve.wait_ge(w_hi_ready, NT * NT + 2 * NT + 1)
            nc.vector.tensor_tensor(bv_split[:, :, 1], bv, bv_split[:, :, 0].bitcast(F32), ALU.subtract)\
                .then_inc(w_lo_ready, 1)
            links["setup"] = links["count"]

            for j in range(NCH):
                take_stats(fixed(0), j)
                take_pool(fixed(0), j)
            dve.wait_ge(consts_ready, 3)
            for u in range(UNITS):
                chain(fixed(0), u)
            split_lo(fixed(0), 0)
            split_lo(fixed(0), 1)
            for j in range(NCH):
                take_stats(fixed(1), j)
                take_pool(fixed(1), j)

            def step(s, with_chain=True, with_stats=True):
                for u in range(UNITS):
                    j, o = divmod(u, NT)
                    if with_chain:
                        chain(following(s, 1), u)
                    if with_stats and u in POOL_AT:
                        take_pool(following(s, 2), POOL_AT[u])
                    if o == NT - 1:
                        if j + 2 < NCH:
                            split_lo(s, j + 2)
                        elif with_chain:
                            split_lo(following(s, 1), j + 2 - NCH)
                        if with_stats:
                            take_stats(following(s, 2), j)

            step(fixed(0))
            with dve.Fori(0, (B - 4) // 2) as i:
                for s in pair(i):
                    step(s)
            step(fixed(B - 3))
            step(fixed(B - 2), with_stats=False)
            step(fixed(B - 1), with_chain=False, with_stats=False)


_INS = ["x", "L0_conv_qk_w", "L0_conv_qk_b", "L0_conv_v_w", "L0_conv_v_b", "L0_conv_proj_w", "L0_conv_proj_b",
        "L0_conv_temperature"]


def kernel(**inputs):
    import numpy as np
    import concourse.bacc as bacc
    from concourse import mybir as mb
    from concourse.bass_utils import run_bass_kernel_spmd as run

    nc = bacc.Bacc("TRN2", target_bir_lowering=False, num_devices=1, dynamic_dma_scratch_size=256)
    arrays, args = {}, []
    for name in _INS:
        a = np.ascontiguousarray(inputs[name])
        arrays[name] = a
        args.append(nc.dram_tensor(name, a.shape, mb.dt.from_np(a.dtype), kind="ExternalInput").ap())
    y = nc.dram_tensor("y", inputs["x"].shape, mb.dt.float32, kind="ExternalOutput").ap()
    conv_attention_program(nc, *args, y)
    r = run(nc, [arrays], core_ids=[0])
    return r.results[0]["y"]
```

```python
from contextlib import ExitStack

import concourse.bass as bass
from concourse import mybir

F32 = mybir.dt.float32
F32R = mybir.dt.float32r
I32 = mybir.dt.int32
ALU = mybir.AluOpType
ACT = mybir.ActivationFunctionType
AX = mybir.AxisListType

P = 128
HEAD = 32
POOL = 2
GROUPS = 32
GN_EPS = 1e-5
NORM_EPS = 1e-12
MASKED = -1e30
RSQRT_MAGIC = float(0x5F3759DF)


def conv_attention_program(nc, x, qk_w, qk_b, v_w, v_b, proj_w, proj_b, temperature, out):
    B, C, H, W = x.shape
    NT = C // P
    HW = H * W
    CH = 512
    NCH = HW // CH
    NPOS = HW // (POOL * POOL)
    PCH = NPOS // NCH
    UNITS = NCH * NT
    GP = (C // GROUPS) // NT
    XSLOTS = 2 * NCH
    CG = C + 2
    KQ = 2 * P
    assert PCH == P and NT == 3 and C % GROUPS == 0 and B % 2 == 0 and NCH == 8

    xv = x.rearrange("b (p t) h w -> b p t (h w)", t=NT)
    ov = out.rearrange("b (p t) h w -> b p t (h w)", t=NT)

    TAKE_AT = {7: 0, 8: 1, 9: 2, 10: 3, 12: 4, 15: 5, 18: 6, 21: 7}

    with ExitStack() as ctx:
        def sb(name, shape, dt=F32):
            return ctx.enter_context(nc.sbuf_tensor(name, shape, dt))

        def sem(name):
            return ctx.enter_context(nc.semaphore(name))

        xs = sb("xs", [P, XSLOTS, NT * CH])
        x_hi = sb("x_hi", [P, 2, NT, CH], F32R)
        x_lo = sb("x_lo", [P, 2, NT, CH], F32R)
        staged = sb("staged", [P, 2, NT, CH])
        wT_hi = sb("wT_hi", [P, NT, NT, KQ], F32R)
        wT_lo = sb("wT_lo", [P, NT, NT, KQ], F32R)
        wv_hi = sb("wv_hi", [P, NT, NT, P], F32R)
        wv_lo = sb("wv_lo", [P, NT, NT, P], F32R)
        wpT = sb("wpT", [P, NT, C])
        pooled = sb("pooled", [P, NT, NPOS])
        m_hi = sb("m_hi", [P, 2, NT, C], F32R)
        m_lo = sb("m_lo", [P, 2, NT, C], F32R)
        g_hi = sb("g_hi", [P, NT, CG], F32R)
        g_lo = sb("g_lo", [P, NT, CG], F32R)
        t_hi = sb("t_hi", [P, NT, KQ + 2], F32R)
        t_lo = sb("t_lo", [P, NT, KQ + 2], F32R)
        xT_hi, xT_lo = [
            t[:, :, :].rearrange("p k c -> p (k c)")[:, 0:2 * CG].rearrange("p (s c) -> p s c", s=2)
            for t in (t_hi, t_lo)]
        work = sb("work", [P, 3 * C])
        bq_row = sb("bq_row", [P, NT, P])
        ident = sb("ident", [P, P])
        own_head = sb("own_head", [P, P])
        group_avg = sb("group_avg", [P, P])
        bn = sb("bn", [P, NCH, 6])
        squares = sb("squares", [P, NT * CH], mybir.dt.bfloat16)
        bv_split = sb("bv_split", [P, NT, 2], F32R)
        small = sb("small", [P, 88])

        st = work[:, 0:C].rearrange("p (b e) -> p b e", b=NT)
        rows = work[:, C:2 * C].rearrange("p (b e) -> p b e", b=NT)
        logits = work[:, 2 * C:3 * C].rearrange("p (b e) -> p b e", b=NT)
        attn = work[:, 0:C].rearrange("p (b e) -> p b e", b=NT)
        m_full = work[:, :].rearrange("p (t o) -> p t o", t=NT)

        cursor = [0]

        def cols(n):
            a = cursor[0]
            cursor[0] += n
            return small[:, a:a + n]

        neg_shift = cols(1)
        sum_squares = cols(NCH)
        all_squares = cols(1)
        pooled_mv = cols(2)
        off_mean = cols(1)
        off_mean2 = cols(1)
        mv = cols(2)
        gmv = cols(2)
        dev = cols(1)
        dev2 = cols(1)
        var = cols(1)
        rstd = cols(1)
        negmean = cols(2)
        pool_scale = cols(1)
        pool_shift = cols(1)
        newton_a = cols(6)
        norm2 = cols(6)
        wsum = cols(6)
        norm_b = cols(6)
        rnorm = cols(6)
        rk_bk = cols(3)
        sum_q = cols(3)
        rq_temp = cols(3)
        neg_max = cols(3)
        exp_sum = cols(3)
        bias_raw = cols(3)
        kq_bias = small[:, 82:88].rearrange("p (s b) -> p s b", s=2)
        kq_bias_flat = small[:, 82:88]
        assert cursor[0] <= 82
        small2 = sb("small2", [P, 21])
        temp = small2[:, 0:3]
        bp = small2[:, 3:6]
        bv = small2[:, 6:9]
        bias = small2[:, 9:15]
        n_bias = small2[:, 15:21]

        main_bank = [ctx.enter_context(nc.psum_tensor(f"main{i}", [P, CH], F32)) for i in range(4)]
        bank_a, bank_b, bank_c, bank_d = [
            ctx.enter_context(nc.psum_tensor(f"chain{i}", [P, CH], F32)) for i in range(4)]

        raw_loaded = sem("raw_loaded")
        small_loaded = sem("small_loaded")
        x_loaded = [sem(f"x_loaded{s}") for s in range(XSLOTS)]
        out_stored = [sem(f"out_stored{s}") for s in range(2)]
        consts_step = sem("consts_step")
        consts_ready = sem("consts_ready")
        ones_ready = sem("ones_ready")
        zeros_ready = sem("zeros_ready")
        w_transposed = sem("w_transposed")
        w_hi_ready = sem("w_hi_ready")
        w_lo_ready = sem("w_lo_ready")
        hi_ready = sem("hi_ready")
        lo_ready = sem("lo_ready")
        unit_done = sem("unit_done")
        evacuated = sem("evacuated")
        vec_step = sem("vec_step")
        act_step = sem("act_step")
        bn_taken = sem("bn_taken")
        shift_ready = sem("shift_ready")
        squares_taken = sem("squares_taken")
        pool_taken = sem("pool_taken")
        stats_ready = sem("stats_ready")
        gmean_done = sem("gmean_done")
        dev_ready = sem("dev_ready")
        gvar_done = sem("gvar_done")
        mean_ready = sem("mean_ready")
        pooled_ready = sem("pooled_ready")
        turned = sem("turned")
        xT_hi_ready = sem("xT_hi_ready")
        xT_lo_ready = sem("xT_lo_ready")
        gram_done = sem("gram_done")
        g_hi_ready = sem("g_hi_ready")
        g_lo_ready = sem("g_lo_ready")
        g_turned = sem("g_turned")
        g_hi_full = sem("g_hi_full")
        g_lo_full = sem("g_lo_full")
        sums_hi_ready = sem("sums_hi_ready")
        sums_lo_ready = sem("sums_lo_ready")
        t_done = sem("t_done")
        t_hi_ready = sem("t_hi_ready")
        t_lo_ready = sem("t_lo_ready")
        s_done = sem("s_done")
        s_read = sem("s_read")
        s_scaled = sem("s_scaled")
        s_turned = sem("s_turned")
        logits_ready = sem("logits_ready")
        exp_done = sem("exp_done")
        attn_ready = sem("attn_ready")
        p1_done = sem("p1_done")
        p1_hi_ready = sem("p1_hi_ready")
        p1_lo_ready = sem("p1_lo_ready")
        m_done = sem("m_done")
        m_scaled = sem("m_scaled")
        m_full_ready = sem("m_full_ready")
        m_hi_ready = sem("m_hi_ready")
        m_ready = sem("m_ready")
        bias_done = sem("bias_done")
        bias_ready = sem("bias_ready")

        def wait_count(eng, semaphore, value):
            if isinstance(value, int) and value <= 0:
                return
            eng.wait_ge(semaphore, value)

        class Step:

            def __init__(self, b, parity, half):
                self.b, self.parity, self.half = b, parity, half

        def fixed(b):
            return Step(b, b % 2, b // 2)

        def following(s, n):
            return Step(s.b + n, (s.parity + n) % 2, s.half + (s.parity + n) // 2)

        def pair(i):
            return Step(2 * i + 1, 1, i), Step(2 * i + 2, 0, i + 1)

        def slot(s, j):
            return NCH * s.parity + j

        raw = xs[:, XSLOTS - 3:XSLOTS, :].rearrange("p s n -> p (s n)")
        raw_qk = raw[:, 0:2 * NT * C].rearrange("p (k c) -> p k c", c=C)
        raw_v = raw[:, 2 * NT * C:3 * NT * C].rearrange("p (k c) -> p k c", c=C)
        raw_p = raw[:, 3 * NT * C:4 * NT * C].rearrange("p (t d) -> p t d", d=C)
        SMALL_LOADS = 4 + 2 + 1 + 1 + 1

        block = ctx.enter_context(nc.Block())

        @block.sync
        def _(sp):
            def load(s, j):
                sp.dma_start(xs[:, slot(s, j), :].rearrange("p (t n) -> p t n", t=NT),
                             xv[bass.ds(s.b, 1), :, :, j * CH:(j + 1) * CH].rearrange(
                                 "a p t n -> p (a t) n")).then_inc(x_loaded[slot(s, j)], 16)

            def store(s, j):
                sp.wait_ge(evacuated, UNITS * s.b + NT * (j + 1))
                sp.dma_start(ov[bass.ds(s.b, 1), :, :, j * CH:(j + 1) * CH].rearrange(
                    "a p t n -> p (a t) n"), staged[:, j % 2, :, :]).then_inc(out_stored[j % 2], 16)

            def reload(s, j):
                n = following(s, (j + 1) // NCH)
                sp.wait_ge(lo_ready, NCH * s.b + j + 2)
                load(following(n, 2), (j + 1) % NCH)

            def step(s, reloads):
                for j in range(NCH):
                    if j < reloads:
                        reload(s, j)
                    store(s, j)

            for j in range(NCH):
                load(fixed(0), j)
            for j in range(NCH - 3):
                load(fixed(1), j)
            sp.wait_ge(w_lo_ready, NT * NT + NT)
            sp.wait_ge(w_hi_ready, NT * NT + 2 * NT)
            for j in range(NCH - 3, NCH):
                load(fixed(1), j)
            sp.wait_ge(lo_ready, 1)
            load(fixed(2), 0)
            step(fixed(0), NCH)
            with sp.Fori(0, (B - 4) // 2) as i:
                for s in pair(i):
                    step(s, NCH)
            step(fixed(B - 3), NCH - 1)
            step(fixed(B - 2), 0)
            step(fixed(B - 1), 0)
            for s in range(2):
                sp.wait_ge(out_stored[s], 16 * B * NCH // 2)

        @block.gpsimd
        def _(pool):
            nc.gpsimd.memset(ident[:, :], 0.0).then_inc(consts_step, 1)
            nc.gpsimd.memset(own_head[:, :], 0.0).then_inc(consts_step, 1)
            nc.gpsimd.memset(group_avg[:, :], 1.0 / GP).then_inc(consts_step, 1)
            pool.wait_ge(consts_step, 3)
            nc.gpsimd.affine_select(out=ident[:, :], in_=ident[:, :], compare_op=ALU.not_equal, fill=1.0,
                                    base=0, pattern=[[-1, P]], channel_multiplier=1).then_inc(consts_ready, 1)
            for m, width, fill in ((own_head, HEAD, MASKED), (group_avg, GP, 0.0)):
                v = m[:, :].rearrange("p (k w) -> p k w", w=width)
                nc.gpsimd.affine_select(out=v, in_=v, compare_op=ALU.is_ge, fill=fill, base=0,
                                        pattern=[[-width, P // width], [0, width]],
                                        channel_multiplier=1).then_inc(consts_step, 1)
            pool.wait_ge(consts_step, 5)
            for m, width, fill in ((own_head, HEAD, MASKED), (group_avg, GP, 0.0)):
                v = m[:, :].rearrange("p (k w) -> p k w", w=width)
                nc.gpsimd.affine_select(out=v, in_=v, compare_op=ALU.is_ge, fill=fill, base=width - 1,
                                        pattern=[[width, P // width], [0, width]],
                                        channel_multiplier=-1).then_inc(consts_ready, 1)

        @block.tensor
        def _(pe):
            def three_passes(dst, lhs, rhs, start, stop, skip=False):
                nc.tensor.matmul(dst, lhs[0], rhs[0], start=start, stop=False, skip_group_check=skip)
                nc.tensor.matmul(dst, lhs[0], rhs[1], start=False, stop=False, skip_group_check=skip)
                return nc.tensor.matmul(dst, lhs[1], rhs[0], start=False, stop=stop, skip_group_check=skip)

            def unit(s, u):
                j, o = divmod(u, NT)
                if u == 0:
                    pe.wait_ge(m_ready, NT * (s.b + 1))
                if o == 0:
                    pe.wait_ge(lo_ready, NCH * s.b + j + 1)
                wait_count(pe, evacuated, UNITS * s.b + u - 3)
                for t in range(NT):
                    last = three_passes(
                        main_bank[u % 4][:, :],
                        (m_hi[:, s.parity, t, o * P:(o + 1) * P], m_lo[:, s.parity, t, o * P:(o + 1) * P]),
                        (x_hi[:, j % 2, t, :], x_lo[:, j % 2, t, :]), t == 0, t == NT - 1)
                last.then_inc(unit_done, 1)

            def group_mean(s):
                pe.wait_ge(stats_ready, s.b + 1)
                wait_count(pe, m_scaled, NT * s.b)
                wait_count(pe, bias_ready, s.b)
                nc.tensor.matmul(bank_c[:, 0:2], group_avg[:, :], mv, start=True, stop=True)\
                    .then_inc(gmean_done, 1)

            def group_var(s):
                pe.wait_ge(dev_ready, s.b + 1)
                nc.tensor.matmul(bank_d[:, 0:1], group_avg[:, :], dev2, start=True, stop=True)\
                    .then_inc(gvar_done, 1)

            def turn(s, c):
                bank = bank_c if c % 2 == 0 else bank_d
                if c % (NCH // 2) == 0:
                    pe.wait_ge(pooled_ready, 2 * s.b + c // (NCH // 2) + 1)
                if c >= 2:
                    pe.wait_ge(xT_hi_ready, NCH * s.b + c - 1)
                    pe.wait_ge(xT_lo_ready, NCH * s.b + c - 1)
                for t in range(NT):
                    last = nc.tensor.transpose(bank[:, t * P:(t + 1) * P],
                                               pooled[:, t, c * PCH:(c + 1) * PCH], ident[:, :])
                last.then_inc(turned, 1)

            def gram(s, c):
                pe.wait_ge(xT_hi_ready, NCH * s.b + c + 1)
                pe.wait_ge(xT_lo_ready, NCH * s.b + c + 1)
                if c == 0:
                    pe.wait_ge(ones_ready, s.b + 1)
                    pe.wait_ge(zeros_ready, s.b + 1)
                h, l = xT_hi[:, c % 2, :], xT_lo[:, c % 2, :]
                first, final = c == 0, c == NCH - 1
                three_passes(bank_a[:, 0:CG], (h[:, 0:P], l[:, 0:P]), (h[:, 0:CG], l[:, 0:CG]), first, final)
                three_passes(bank_b[:, 0:CG - P], (h[:, P:2 * P], l[:, P:2 * P]),
                             (h[:, P:CG], l[:, P:CG]), first, final, skip=True)
                three_passes(bank_b[:, CG - P:2 * CG - 3 * P], (h[:, 2 * P:3 * P], l[:, 2 * P:3 * P]),
                             (h[:, 2 * P:CG], l[:, 2 * P:CG]), False, final, skip=True)\
                    .then_inc(gram_done, 1)

            def turn_gram(s):
                for ready, g, bank in ((g_hi_ready, g_hi, bank_c), (g_lo_ready, g_lo, bank_d)):
                    pe.wait_ge(ready, s.b + 1)
                    if bank is bank_c:
                        pe.wait_ge(xT_hi_ready, NCH * (s.b + 1))
                        pe.wait_ge(xT_lo_ready, NCH * (s.b + 1))
                    for n, (row, col) in enumerate(((0, 1), (0, 2), (1, 2))):
                        last = nc.tensor.transpose(bank[:, n * P:(n + 1) * P],
                                                   g[:, row, col * P:(col + 1) * P].bitcast(F32), ident[:, :])
                    last.then_inc(g_turned, 1)

            def t_block(s, blk):
                if blk == 0:
                    pe.wait_ge(g_hi_full, s.b + 1)
                    pe.wait_ge(g_lo_full, s.b + 1)
                else:
                    pe.wait_ge(t_hi_ready, NT * s.b + blk)
                    pe.wait_ge(t_lo_ready, NT * s.b + blk)
                for i, dst in enumerate((bank_a[:, 0:KQ], bank_a[:, KQ:2 * KQ], bank_b[:, 0:KQ])):
                    for k in range(NT):
                        last = three_passes(dst, (g_hi[:, k, i * P:(i + 1) * P], g_lo[:, k, i * P:(i + 1) * P]),
                                            (wT_hi[:, k, blk, :], wT_lo[:, k, blk, :]), k == 0, k == NT - 1)
                last.then_inc(t_done, 1)

            def s_block(s, blk):
                pe.wait_ge(t_hi_ready, NT * s.b + blk + 1)
                pe.wait_ge(t_lo_ready, NT * s.b + blk + 1)
                if blk == 0:
                    pe.wait_ge(sums_hi_ready, s.b + 1)
                    pe.wait_ge(sums_lo_ready, s.b + 1)
                if blk == 2:
                    pe.wait_ge(s_read, NT * s.b + 1)
                bank = bank_d if blk == 1 else bank_c
                for w0, dst, c0 in ((0, bank[:, 0:KQ + 2], 0), (P, bank[:, KQ + 2:KQ + 2 + P + 2], P)):
                    for k in range(NT):
                        last = three_passes(dst, (wT_hi[:, k, blk, w0:w0 + P], wT_lo[:, k, blk, w0:w0 + P]),
                                            (t_hi[:, k, c0:KQ + 2], t_lo[:, k, c0:KQ + 2]), k == 0, k == NT - 1)
                last.then_inc(s_done, 1)

            def turn_scores(s):
                pe.wait_ge(s_scaled, s.b + 1)
                for src, bank in ((st, bank_c), (rows, bank_d)):
                    for blk in range(NT):
                        last = nc.tensor.transpose(bank[:, blk * P:(blk + 1) * P], src[:, blk, :], ident[:, :])
                last.then_inc(s_turned, 1)

            def fold_proj(s):
                pe.wait_ge(attn_ready, s.b + 1)
                for blk, bank in enumerate((bank_a, bank_b, bank_d)):
                    nc.tensor.matmul(bank[:, 0:C], attn[:, blk, :], wpT[:, blk, :], start=True, stop=True)\
                        .then_inc(p1_done, 1)

            def fold_value(s):
                pe.wait_ge(p1_hi_ready, NT * (s.b + 1))
                pe.wait_ge(p1_lo_ready, NT * (s.b + 1))
                for t, bank in enumerate((bank_c, bank_a, bank_b)):
                    for blk in range(NT):
                        last = three_passes(bank[:, 0:C], (wv_hi[:, blk, t, :], wv_lo[:, blk, t, :]),
                                            (g_hi[:, blk, 0:C], g_lo[:, blk, 0:C]), blk == 0, blk == NT - 1)
                    last.then_inc(m_done, 1)
                for o in range(NT):
                    for blk in range(NT):
                        for part, g in enumerate((g_hi, g_lo)):
                            last = nc.tensor.matmul(bank_d[:, 2 * o:2 * o + 2], g[:, blk, o * P:(o + 1) * P],
                                                    bv_split[:, blk, :], start=(blk == 0 and part == 0),
                                                    stop=(blk == NT - 1 and part == 1))
                last.then_inc(bias_done, 1)

            def chain(s, u):
                if u == 0:
                    group_mean(s)
                if u == 1:
                    group_var(s)
                if 4 <= u <= 7:
                    gram(s, 2 * (u - 4))
                    gram(s, 2 * (u - 4) + 1)
                if 3 <= u <= 6:
                    turn(s, 2 * (u - 3))
                    turn(s, 2 * (u - 3) + 1)
                if u == 8:
                    turn_gram(s)
                if 10 <= u <= 12:
                    s_block(s, u - 10)
                if 9 <= u <= 11:
                    t_block(s, u - 9)
                if u == 14:
                    turn_scores(s)
                if u == 17:
                    fold_proj(s)
                if u == 19:
                    fold_value(s)

            pe.wait_ge(consts_ready, 3)
            pe.wait_ge(raw_loaded, 16 * 3)
            n = 0
            for blk in range(NT):
                for t in range(NT):
                    bank = main_bank[n % 4]
                    if n >= 4:
                        pe.wait_ge(w_hi_ready, n - 3)
                        pe.wait_ge(w_lo_ready, n - 3)
                    for half, row in ((0, NT + blk), (1, blk)):
                        last = nc.tensor.transpose(bank[:, half * P:(half + 1) * P],
                                                   raw_qk[:, row, :].rearrange("p (c t) -> p t c", t=NT)[:, t, :],
                                                   ident[:, :])
                    last.then_inc(w_transposed, 1)
                    n += 1
            for blk in range(NT):
                bank = (bank_a, bank_b, bank_c)[blk]
                for t in range(NT):
                    last = nc.tensor.transpose(bank[:, t * P:(t + 1) * P],
                                               raw_p[:, t, blk * P:(blk + 1) * P], ident[:, :])
                last.then_inc(w_transposed, 1)
            pe.wait_ge(w_hi_ready, NT * NT + 2 * NT)
            pe.wait_ge(w_lo_ready, NT * NT + NT)
            for u in range(UNITS):
                chain(fixed(0), u)

            def step(s, with_chain=True):
                for u in range(UNITS):
                    if with_chain:
                        chain(following(s, 1), u)
                    unit(s, u)

            step(fixed(0))
            with pe.Fori(0, (B - 2) // 2) as i:
                for s in pair(i):
                    step(s)
            step(fixed(B - 1), with_chain=False)

        @block.scalar
        def _(act):
            def split_hi(s, j):
                act.wait_ge(x_loaded[slot(s, j)], 16 * (s.half + 1))
                if j < 2:
                    act.wait_ge(mean_ready, s.b + 1)
                wait_count(act, unit_done, UNITS * s.b + NT * (j - 1))
                nc.scalar.activation(x_hi[:, j % 2, :, :].rearrange("p t n -> p (t n)"), xs[:, slot(s, j), :],
                                     ACT.Identity, bias=negmean[:, s.parity:s.parity + 1]).then_inc(hi_ready, 1)

            def evacuate(s, u):
                j, o = divmod(u, NT)
                if u == 0:
                    act.wait_ge(bias_ready, s.b + 1)
                if o == 0:
                    wait_count(act, out_stored[j % 2], 16 * ((NCH // 2) * s.b + j // 2))
                act.wait_ge(unit_done, UNITS * s.b + u + 1)
                nc.scalar.activation(staged[:, j % 2, o, :], main_bank[u % 4][:, :], ACT.Identity,
                                     bias=bias[:, NT * s.parity + o:NT * s.parity + o + 1]).then_inc(evacuated, 1)

            def take_squares(s, j):
                act.wait_ge(x_loaded[slot(s, j)], 16 * (s.half + 1))
                if j == 0:
                    act.wait_ge(shift_ready, s.b + 1)
                    wait_count(act, stats_ready, s.b)
                wait_count(act, squares_taken, NCH * s.b + j)
                nc.scalar.activation(squares[:, :], xs[:, slot(s, j), :], ACT.Square, bias=neg_shift,
                                     accum_out=sum_squares[:, j:j + 1]).then_inc(squares_taken, 1)

            def xT_high(s, c):
                act.wait_ge(turned, NCH * s.b + c + 1)
                if c >= 2:
                    act.wait_ge(gram_done, NCH * s.b + c - 1)
                else:
                    wait_count(act, s_done, NT * s.b)
                bank = bank_c if c % 2 == 0 else bank_d
                nc.scalar.activation(xT_hi[:, c % 2, 0:C], bank[:, 0:C], ACT.Copy).then_inc(xT_hi_ready, 1)

            def gram_high(s):
                act.wait_ge(gram_done, NCH * (s.b + 1))
                nc.scalar.activation(g_hi[:, 0, :], bank_a[:, 0:CG], ACT.Copy)
                nc.scalar.activation(g_hi[:, 1, P:CG], bank_b[:, 0:CG - P], ACT.Copy)
                nc.scalar.activation(g_hi[:, 2, 2 * P:CG], bank_b[:, CG - P:2 * CG - 3 * P], ACT.Copy)\
                    .then_inc(g_hi_ready, 1)

            def gram_high_lower(s):
                act.wait_ge(g_turned, 2 * s.b + 1)
                nc.scalar.activation(g_hi[:, 1, 0:P], bank_c[:, 0:P], ACT.Copy)
                nc.scalar.activation(g_hi[:, 2, 0:2 * P], bank_c[:, P:3 * P], ACT.Copy).then_inc(g_hi_full, 1)
                act.wait_ge(g_hi_ready, s.b + 1)
                wait_count(act, s_done, NT * s.b)
                nc.scalar.activation(t_hi[:, :, KQ:KQ + 2], g_hi[:, :, C:CG].bitcast(F32), ACT.Copy)\
                    .then_inc(sums_hi_ready, 1)

            def t_high(s, blk):
                act.wait_ge(t_done, NT * s.b + blk + 1)
                if blk == 0:
                    wait_count(act, s_done, NT * s.b)
                nc.scalar.activation(t_hi[:, 0:2, 0:KQ], bank_a[:, :].rearrange("p (i c) -> p i c", i=2), ACT.Copy)
                nc.scalar.activation(t_hi[:, 2, 0:KQ], bank_b[:, 0:KQ], ACT.Copy).then_inc(t_hi_ready, 1)

            def exps(s):
                act.wait_ge(logits_ready, s.b + 1)
                for blk in range(NT):
                    last = nc.scalar.activation(attn[:, blk, :], logits[:, blk, :], ACT.Exp,
                                                bias=neg_max[:, blk:blk + 1], accum_out=exp_sum[:, blk:blk + 1])
                last.then_inc(exp_done, 1)

            def p1_high(s):
                for blk, bank in enumerate((bank_a, bank_b, bank_d)):
                    act.wait_ge(p1_done, NT * s.b + blk + 1)
                    nc.scalar.activation(g_hi[:, blk, 0:C], bank[:, 0:C], ACT.Copy).then_inc(p1_hi_ready, 1)

            def scale_m(s):
                for t, bank in enumerate((bank_c, bank_a, bank_b)):
                    act.wait_ge(m_done, NT * s.b + t + 1)
                    nc.scalar.activation(m_full[:, t, :], bank[:, 0:C], ACT.Copy, scale=rstd).then_inc(m_scaled, 1)

            def m_high(s):
                for t in range(NT):
                    act.wait_ge(m_full_ready, NT * s.b + t + 1)
                    nc.scalar.activation(m_hi[:, s.parity, t, :], m_full[:, t, :], ACT.Copy).then_inc(m_hi_ready, 1)

            def chain(s, u):
                if 3 <= u <= 6:
                    xT_high(s, 2 * (u - 3))
                    xT_high(s, 2 * (u - 3) + 1)
                if u == 7:
                    gram_high(s)
                if u == 8:
                    gram_high_lower(s)
                if 9 <= u <= 11:
                    t_high(s, u - 9)
                if u == 16:
                    exps(s)
                if u == 17:
                    p1_high(s)
                if u == 19:
                    scale_m(s)
                    m_high(s)

            act.dma_start(raw_qk, qk_w.rearrange("(k p) c -> p k c", p=P)).then_inc(raw_loaded, 16)
            act.dma_start(raw_v, v_w.rearrange("(k p) c -> p k c", p=P)).then_inc(raw_loaded, 16)
            act.dma_start(raw_p, proj_w.rearrange("(p t) d -> p t d", t=NT)).then_inc(raw_loaded, 16)
            with nc.allow_non_contiguous_dma(reason="a few hundred single words, once"):
                for hh in range(4):
                    act.dma_start(temp[HEAD * hh:HEAD * (hh + 1), :],
                                 temperature.rearrange("(b h) x y -> h (b x y)", h=4)[hh:hh + 1, :]
                                 .to_broadcast([HEAD, NT])).then_inc(small_loaded, 16)
                for k in range(2):
                    act.dma_start(kq_bias[:, 1 - k, :], qk_b[k * C:(k + 1) * C].rearrange("(b p) -> p b", p=P))\
                        .then_inc(small_loaded, 16)
                act.dma_start(bv, v_b.rearrange("(b p) -> p b", p=P)).then_inc(small_loaded, 16)
                act.dma_start(bp, proj_b.rearrange("(p t) -> p t", t=NT)).then_inc(small_loaded, 16)
                act.dma_start(bq_row[:, :, :].rearrange("p b e -> p (b e)"),
                             qk_b[0:C].rearrange("(a n) -> a n", a=1).to_broadcast([P, C])).then_inc(small_loaded, 16)
            for j in range(NCH):
                take_squares(fixed(0), j)
            for n in range(NT * NT):
                blk, t = divmod(n, NT)
                act.wait_ge(w_transposed, n + 1)
                nc.scalar.activation(wT_hi[:, t, blk, :], main_bank[n % 4][:, 0:KQ], ACT.Copy)\
                    .then_inc(w_hi_ready, 1)
            for blk, bank in enumerate((bank_a, bank_b, bank_c)):
                act.wait_ge(w_transposed, NT * NT + blk + 1)
                nc.scalar.activation(wpT[:, blk, :], bank[:, 0:C], ACT.Copy).then_inc(w_hi_ready, 1)
            for blk in range(NT):
                nc.scalar.activation(wv_hi[:, blk, :, :], raw_v[:, blk, :].rearrange("p (c t) -> p t c", t=NT),
                                     ACT.Copy).then_inc(w_hi_ready, 1)
            act.wait_ge(small_loaded, 16 * SMALL_LOADS)
            nc.scalar.activation(bv_split[:, :, 0], bv, ACT.Copy).then_inc(w_hi_ready, 1)

            for u in range(UNITS):
                chain(fixed(0), u)
            split_hi(fixed(0), 0)
            split_hi(fixed(0), 1)

            def step(s, with_chain=True, with_squares=True):
                for u in range(UNITS):
                    if with_chain:
                        chain(following(s, 1), u)
                    evacuate(s, u)
                    j, o = divmod(u, NT)
                    if o == NT - 1:
                        if j + 2 < NCH:
                            split_hi(s, j + 2)
                        elif with_chain:
                            split_hi(following(s, 1), j + 2 - NCH)
                    if with_squares and u in TAKE_AT:
                        take_squares(following(s, 2), TAKE_AT[u])

            for j in range(NCH):
                take_squares(fixed(1), j)
            step(fixed(0))
            with act.Fori(0, (B - 4) // 2) as i:
                for s in pair(i):
                    step(s)
            step(fixed(B - 3))
            step(fixed(B - 2), with_squares=False)
            step(fixed(B - 1), with_chain=False, with_squares=False)

        @block.vector
        def _(dve):
            links = {"base": 0, "count": 0, "setup": 0, "per_image": None}

            def link(ins):
                links["count"] += 1
                ins.then_inc(vec_step, 1)
                dve.wait_ge(vec_step, links["base"] + links["count"])

            def open_links(s):
                links["count"] = 0
                links["base"] = links["setup"] + (0 if links["per_image"] is None else links["per_image"] * s.b)

            def close_links():
                assert links["per_image"] in (None, links["count"])
                links["per_image"] = links["count"]

            def rsqrt(y, v):
                a = newton_a[:, 0:v.shape[1]]
                link(nc.vector.tensor_scalar(a.bitcast(I32), v.bitcast(I32), 1, None, ALU.logical_shift_right))
                link(nc.vector.tensor_scalar(y.bitcast(I32), a.bitcast(I32), -1.0, RSQRT_MAGIC, ALU.mult, ALU.add))
                for _ in range(3):
                    link(nc.vector.scalar_tensor_tensor(out=a, in0=y, scalar=-0.5, in1=v,
                                                        op0=ALU.mult, op1=ALU.mult))
                    link(nc.vector.tensor_tensor(a, a, y, ALU.mult))
                    link(nc.vector.scalar_tensor_tensor(out=y, in0=a, scalar=1.5, in1=y,
                                                        op0=ALU.add, op1=ALU.mult))

            def split_lo(s, j):
                dve.wait_ge(hi_ready, NCH * s.b + j + 1)
                nc.vector.scalar_tensor_tensor(
                    out=x_lo[:, j % 2, :, :].rearrange("p t n -> p (t n)"), in0=xs[:, slot(s, j), :],
                    scalar=negmean[:, s.parity:s.parity + 1],
                    in1=x_hi[:, j % 2, :, :].rearrange("p t n -> p (t n)").bitcast(F32),
                    op0=ALU.add, op1=ALU.subtract).then_inc(lo_ready, 1)

            def take_pool(s, j):
                dve.wait_ge(x_loaded[slot(s, j)], 16 * (s.half + 1))
                if j == 0:
                    wait_count(dve, turned, NCH * s.b)
                quads = xs[:, slot(s, j), :].rearrange("p (r a c w) -> p r c a w", a=POOL, w=POOL, c=W // POOL)
                dst = pooled[:, :, j * PCH:(j + 1) * PCH]
                nc.vector.tensor_reduce(dst, quads, AX.XY, ALU.add).then_inc(pool_taken, 1)
                dve.wait_ge(pool_taken, NCH * s.b + j + 1)
                nc.vector.bn_stats(bn[:, j, :], dst).then_inc(bn_taken, 1)
                if j == 0:
                    dve.wait_ge(bn_taken, NCH * s.b + 1)
                    nc.vector.tensor_scalar(neg_shift, bn[:, 0, 1:2], -1.0 / (POOL * POOL), None, ALU.mult)\
                        .then_inc(shift_ready, 1)

            def partition_stats(s):
                n = float(NT * HW)
                dve.wait_ge(bn_taken, NCH * (s.b + 1))
                nc.vector.memset(dev, 0.0)
                link(nc.vector.bn_aggr(pooled_mv, bn[:, :, :].rearrange("p k s -> p (k s)")))
                link(nc.vector.scalar_tensor_tensor(out=off_mean, in0=pooled_mv[:, 0:1], scalar=1.0 / (POOL * POOL),
                                                    in1=neg_shift, op0=ALU.mult, op1=ALU.add))
                dve.wait_ge(squares_taken, NCH * (s.b + 1))
                link(nc.vector.tensor_reduce(all_squares, sum_squares, AX.X, ALU.add))
                link(nc.vector.tensor_tensor(off_mean2, off_mean, off_mean, ALU.mult))
                link(nc.vector.tensor_scalar(mv[:, 0:1], pooled_mv[:, 0:1], 1.0 / (POOL * POOL), None, ALU.mult))
                nc.vector.scalar_tensor_tensor(out=mv[:, 1:2], in0=all_squares, scalar=1.0 / n, in1=off_mean2,
                                               op0=ALU.mult, op1=ALU.subtract).then_inc(stats_ready, 1)

            def group_dev(s):
                dve.wait_ge(gmean_done, s.b + 1)
                dve.wait_ge(stats_ready, s.b + 1)
                link(nc.vector.tensor_copy(gmv, bank_c[:, 0:2]))
                link(nc.vector.tensor_tensor(dev, mv[:, 0:1], gmv[:, 0:1], ALU.subtract))
                nc.vector.tensor_tensor(dev2, dev, dev, ALU.mult).then_inc(dev_ready, 1)

            def group_scale(s):
                dve.wait_ge(gvar_done, s.b + 1)
                link(nc.vector.scalar_tensor_tensor(out=var, in0=bank_d[:, 0:1], scalar=GN_EPS, in1=gmv[:, 1:2],
                                                    op0=ALU.add, op1=ALU.add))
                rsqrt(rstd, var)
                nm = negmean[:, s.parity:s.parity + 1]
                link(nc.vector.tensor_scalar(nm, gmv[:, 0:1], -1.0, None, ALU.mult))
                link(nc.vector.tensor_scalar(pool_scale, rstd, 1.0 / (POOL * POOL), None, ALU.mult))
                nc.vector.tensor_tensor(pool_shift, nm, rstd, ALU.mult).then_inc(mean_ready, 1)
                dve.wait_ge(mean_ready, s.b + 1)
                dve.wait_ge(pool_taken, NCH * (s.b + 1))
                for half in range(2):
                    v = pooled[:, :, half * NPOS // 2:(half + 1) * NPOS // 2]
                    nc.vector.tensor_scalar(v, v, pool_scale, pool_shift, ALU.mult, ALU.add)\
                        .then_inc(pooled_ready, 1)

            def constant_columns(s):
                wait_count(dve, s_done, NT * s.b)
                nc.vector.memset(xT_hi[:, :, C:CG].bitcast(F32), 1.0).then_inc(ones_ready, 1)
                nc.vector.memset(xT_lo[:, :, C:CG].bitcast(F32), 0.0).then_inc(zeros_ready, 1)

            def xT_low(s, c):
                dve.wait_ge(xT_hi_ready, NCH * s.b + c + 1)
                bank = bank_c if c % 2 == 0 else bank_d
                nc.vector.tensor_tensor(xT_lo[:, c % 2, 0:C], bank[:, 0:C], xT_hi[:, c % 2, 0:C].bitcast(F32),
                                        ALU.subtract).then_inc(xT_lo_ready, 1)

            def gram_low(s):
                dve.wait_ge(g_hi_ready, s.b + 1)
                for i, src in ((0, bank_a[:, 0:CG]), (1, bank_b[:, 0:CG - P]), (2, bank_b[:, CG - P:2 * CG - 3 * P])):
                    last = nc.vector.tensor_tensor(g_lo[:, i, i * P:CG], src, g_hi[:, i, i * P:CG].bitcast(F32),
                                                   ALU.subtract)
                last.then_inc(g_lo_ready, 1)

            def gram_low_lower(s):
                dve.wait_ge(g_turned, 2 * s.b + 2)
                nc.vector.tensor_copy(g_lo[:, 1, 0:P], bank_d[:, 0:P])
                nc.vector.tensor_copy(g_lo[:, 2, 0:2 * P], bank_d[:, P:3 * P]).then_inc(g_lo_full, 1)
                dve.wait_ge(g_lo_ready, s.b + 1)
                wait_count(dve, s_done, NT * s.b)
                nc.vector.tensor_copy(t_lo[:, :, KQ:KQ + 2], g_lo[:, :, C:CG]).then_inc(sums_lo_ready, 1)

            def t_low(s, blk):
                dve.wait_ge(t_hi_ready, NT * s.b + blk + 1)
                nc.vector.tensor_tensor(t_lo[:, 0:2, 0:KQ], bank_a[:, :].rearrange("p (i c) -> p i c", i=2),
                                        t_hi[:, 0:2, 0:KQ].bitcast(F32), ALU.subtract)
                nc.vector.tensor_tensor(t_lo[:, 2, 0:KQ], bank_b[:, 0:KQ], t_hi[:, 2, 0:KQ].bitcast(F32),
                                        ALU.subtract).then_inc(t_lo_ready, 1)

            def read_scores(s, blk):
                dve.wait_ge(s_done, NT * s.b + blk + 1)
                if blk == 0:
                    wait_count(dve, m_ready, NT * s.b)
                bank = bank_d if blk == 1 else bank_c
                link(nc.vector.tensor_copy(wsum.rearrange("p (s b) -> p s b", s=2)[:, :, blk],
                                           bank[:, KQ:KQ + P + 3:P + 2]))
                nc.vector.scalar_tensor_tensor(out=st[:, blk, :], in0=bq_row[:, blk, :], scalar=wsum[:, blk:blk + 1],
                                               in1=bank[:, P:2 * P], op0=ALU.mult, op1=ALU.add)
                nc.vector.scalar_tensor_tensor(out=rows[:, blk, :], in0=bank[:, 0:P], scalar=1.0, in1=ident[:, :],
                                               op0=ALU.mult, op1=ALU.mult, accum_out=norm2[:, blk:blk + 1])
                nc.vector.scalar_tensor_tensor(out=logits[:, blk, :], in0=bank[:, KQ + 2:KQ + 2 + P], scalar=1.0,
                                               in1=ident[:, :], op0=ALU.mult, op1=ALU.mult,
                                               accum_out=norm2[:, NT + blk:NT + blk + 1]).then_inc(s_read, 1)

            def scale_scores(s):
                dve.wait_ge(s_read, NT * (s.b + 1))
                link(nc.vector.scalar_tensor_tensor(out=norm_b, in0=wsum, scalar=2.0, in1=n_bias,
                                                    op0=ALU.mult, op1=ALU.add))
                link(nc.vector.tensor_tensor(norm_b, norm_b, kq_bias_flat, ALU.mult))
                link(nc.vector.tensor_tensor(norm_b, norm_b, norm2, ALU.add))
                link(nc.vector.tensor_scalar(norm_b, norm_b, NORM_EPS * NORM_EPS, None, ALU.max))
                rsqrt(rnorm, norm_b)
                link(nc.vector.tensor_tensor(rk_bk, rnorm[:, 0:NT], kq_bias_flat[:, 0:NT], ALU.mult))
                nc.vector.tensor_tensor(st, st, rnorm[:, 0:NT].unsqueeze(2).to_broadcast([P, NT, P]), ALU.mult)
                nc.vector.tensor_copy(rows, rk_bk.unsqueeze(2).to_broadcast([P, NT, P])).then_inc(s_scaled, 1)
                link(nc.vector.tensor_tensor(sum_q, wsum[:, NT:2 * NT], n_bias[:, NT:2 * NT], ALU.add))
                link(nc.vector.tensor_tensor(rq_temp, rnorm[:, NT:2 * NT], temp, ALU.mult))

            def make_logits(s):
                dve.wait_ge(s_turned, s.b + 1)
                v = [bank[:, 0:C].rearrange("p (b e) -> p b e", b=NT) for bank in (bank_c, bank_d)]
                link(nc.vector.tensor_tensor(rows, v[1], sum_q.unsqueeze(2).to_broadcast([P, NT, P]), ALU.mult))
                link(nc.vector.tensor_tensor(rows, v[0], rows, ALU.add))
                for blk in range(NT):
                    last = nc.vector.scalar_tensor_tensor(out=logits[:, blk, :], in0=rows[:, blk, :],
                                                          scalar=rq_temp[:, blk:blk + 1], in1=own_head[:, :],
                                                          op0=ALU.mult, op1=ALU.add)
                link(last)
                nc.vector.tensor_reduce(neg_max, logits, AX.X, ALU.max, negate=True).then_inc(logits_ready, 1)

            def normalise_attn(s):
                dve.wait_ge(exp_done, s.b + 1)
                link(nc.vector.reciprocal(exp_sum, exp_sum))
                nc.vector.tensor_tensor(attn, attn, exp_sum.unsqueeze(2).to_broadcast([P, NT, P]), ALU.mult)\
                    .then_inc(attn_ready, 1)

            def p1_low(s):
                for blk, bank in enumerate((bank_a, bank_b, bank_d)):
                    dve.wait_ge(p1_hi_ready, NT * s.b + blk + 1)
                    nc.vector.tensor_tensor(g_lo[:, blk, 0:C], bank[:, 0:C], g_hi[:, blk, 0:C].bitcast(F32),
                                            ALU.subtract).then_inc(p1_lo_ready, 1)

            def add_identity(s):
                for t in range(NT):
                    dve.wait_ge(m_scaled, NT * s.b + t + 1)
                    d = m_full[:, t, t * P:(t + 1) * P]
                    nc.vector.tensor_tensor(d, d, ident[:, :], ALU.add).then_inc(m_full_ready, 1)

            def m_low(s):
                for t in range(NT):
                    dve.wait_ge(m_hi_ready, NT * s.b + t + 1)
                    nc.vector.tensor_tensor(m_lo[:, s.parity, t, :], m_full[:, t, :],
                                            m_hi[:, s.parity, t, :].bitcast(F32), ALU.subtract).then_inc(m_ready, 1)

            def make_bias(s):
                dve.wait_ge(bias_done, s.b + 1)
                link(nc.vector.tensor_reduce(bias_raw, bank_d[:, 0:2 * NT].rearrange("p (o h) -> p o h", h=2),
                                             AX.X, ALU.add))
                nc.vector.scalar_tensor_tensor(out=bias[:, NT * s.parity:NT * (s.parity + 1)], in0=bias_raw,
                                               scalar=gmv[:, 0:1], in1=bp, op0=ALU.add, op1=ALU.add)\
                    .then_inc(bias_ready, 1)

            def chain(s, u):
                if u == 0:
                    open_links(s)
                    partition_stats(s)
                    group_dev(s)
                    constant_columns(s)
                if u == 1:
                    group_scale(s)
                if 3 <= u <= 6:
                    xT_low(s, 2 * (u - 3))
                    xT_low(s, 2 * (u - 3) + 1)
                if u == 7:
                    gram_low(s)
                if u == 8:
                    gram_low_lower(s)
                if 9 <= u <= 11:
                    t_low(s, u - 9)
                if 10 <= u <= 12:
                    read_scores(s, u - 10)
                if u == 12:
                    scale_scores(s)
                if u == 14:
                    make_logits(s)
                if u == 16:
                    normalise_attn(s)
                if u == 17:
                    p1_low(s)
                if u == 19:
                    add_identity(s)
                    m_low(s)
                    make_bias(s)
                    close_links()

            for j in range(NCH):
                take_pool(fixed(0), j)
            dve.wait_ge(small_loaded, 16 * SMALL_LOADS)
            link(nc.vector.tensor_scalar(n_bias, kq_bias_flat, float(NPOS), None, ALU.mult))
            for n in range(NT * NT):
                blk, t = divmod(n, NT)
                dve.wait_ge(w_hi_ready, n + 1)
                nc.vector.tensor_tensor(wT_lo[:, t, blk, :], main_bank[n % 4][:, 0:KQ],
                                        wT_hi[:, t, blk, :].bitcast(F32), ALU.subtract).then_inc(w_lo_ready, 1)
            for blk in range(NT):
                dve.wait_ge(w_hi_ready, NT * NT + NT + blk + 1)
                nc.vector.tensor_tensor(wv_lo[:, blk, :, :], raw_v[:, blk, :].rearrange("p (c t) -> p t c", t=NT),
                                        wv_hi[:, blk, :, :].bitcast(F32), ALU.subtract).then_inc(w_lo_ready, 1)
            dve.wait_ge(w_hi_ready, NT * NT + 2 * NT + 1)
            nc.vector.tensor_tensor(bv_split[:, :, 1], bv, bv_split[:, :, 0].bitcast(F32), ALU.subtract)\
                .then_inc(w_lo_ready, 1)
            links["setup"] = links["count"]

            dve.wait_ge(consts_ready, 3)
            for u in range(UNITS):
                chain(fixed(0), u)
            split_lo(fixed(0), 0)
            split_lo(fixed(0), 1)
            for j in range(NCH):
                take_pool(fixed(1), j)

            def step(s, with_chain=True, with_stats=True):
                for u in range(UNITS):
                    j, o = divmod(u, NT)
                    if with_chain:
                        chain(following(s, 1), u)
                    if o == NT - 1:
                        if j + 2 < NCH:
                            split_lo(s, j + 2)
                        elif with_chain:
                            split_lo(following(s, 1), j + 2 - NCH)
                    if with_stats and u in TAKE_AT:
                        take_pool(following(s, 2), TAKE_AT[u])

            step(fixed(0))
            with dve.Fori(0, (B - 4) // 2) as i:
                for s in pair(i):
                    step(s)
            step(fixed(B - 3))
            step(fixed(B - 2), with_stats=False)
            step(fixed(B - 1), with_chain=False, with_stats=False)


_INS = ["x", "L0_conv_qk_w", "L0_conv_qk_b", "L0_conv_v_w", "L0_conv_v_b", "L0_conv_proj_w", "L0_conv_proj_b",
        "L0_conv_temperature"]


def kernel(**inputs):
    import numpy as np
    import concourse.bacc as bacc
    from concourse import mybir as mb
    from concourse.bass_utils import run_bass_kernel_spmd as run

    nc = bacc.Bacc("TRN2", target_bir_lowering=False, num_devices=1, dynamic_dma_scratch_size=256)
    arrays, args = {}, []
    for name in _INS:
        a = np.ascontiguousarray(inputs[name])
        arrays[name] = a
        args.append(nc.dram_tensor(name, a.shape, mb.dt.from_np(a.dtype), kind="ExternalInput").ap())
    y = nc.dram_tensor("y", inputs["x"].shape, mb.dt.float32, kind="ExternalOutput").ap()
    conv_attention_program(nc, *args, y)
    r = run(nc, [arrays], core_ids=[0])
    return r.results[0]["y"]
```

```python
from contextlib import ExitStack

import concourse.bass as bass
from concourse import mybir

F32 = mybir.dt.float32
F32R = mybir.dt.float32r
I32 = mybir.dt.int32
ALU = mybir.AluOpType
ACT = mybir.ActivationFunctionType
AX = mybir.AxisListType

P = 128
HEAD = 32
POOL = 2
GROUPS = 32
GN_EPS = 1e-5
NORM_EPS = 1e-12
MASKED = -1e30
RSQRT_MAGIC = float(0x5F3759DF)


def conv_attention_program(nc, x, qk_w, qk_b, v_w, v_b, proj_w, proj_b, temperature, out):
    B, C, H, W = x.shape
    NT = C // P
    HW = H * W
    CH = 512
    NCH = HW // CH
    NPOS = HW // (POOL * POOL)
    PCH = NPOS // NCH
    UNITS = NCH * NT
    GP = (C // GROUPS) // NT
    XSLOTS = 2 * NCH
    CG = C + 2
    KQ = 2 * P
    assert PCH == P and NT == 3 and C % GROUPS == 0 and B % 2 == 0 and NCH == 8

    xv = x.rearrange("b (p t) h w -> b p t (h w)", t=NT)
    ov = out.rearrange("b (p t) h w -> b p t (h w)", t=NT)

    POOL_AT = {0: 0, 3: 1, 7: 2, 9: 3, 10: 4, 14: 5, 17: 6, 20: 7}
    SHIFT_AT = 3
    SQUARES_AT = {3: 0, 7: 1, 9: 2, 12: 3, 15: 4, 17: 5, 20: 6, 22: 7}
    TURN_AT = {5: 0, 8: 1, 9: 2, 12: 3, 14: 4, 17: 5, 20: 6, 22: 7}
    GRAM_AT = {8: 0, 10: 1, 11: 2, 14: 3, 16: 4, 19: 5, 22: 6, 23: 7}
    FIRST_SPLIT_AT = {9: 0, 14: 1}
    GROUP_AT, SPLIT_GRAM_AT = 1, 3
    T_AT = {7: 0, 9: 1, 11: 2}
    S_AT = {10: 0, 11: 1, 12: 2}
    LOGITS_AT, SOFTMAX_AT, PROJ_AT, VALUE_AT = 16, 17, 19, 21

    with ExitStack() as ctx:
        def sb(name, shape, dt=F32):
            return ctx.enter_context(nc.sbuf_tensor(name, shape, dt))

        def sem(name):
            return ctx.enter_context(nc.semaphore(name))

        xs = sb("xs", [P, XSLOTS, NT * CH])
        x_hi = sb("x_hi", [P, 2, NT, CH], F32R)
        x_lo = sb("x_lo", [P, 2, NT, CH], F32R)
        staged = sb("staged", [P, 2, NT, CH])
        wT_hi = sb("wT_hi", [P, NT, NT, KQ], F32R)
        wT_lo = sb("wT_lo", [P, NT, NT, KQ], F32R)
        wv_hi = sb("wv_hi", [P, NT, NT, P], F32R)
        wv_lo = sb("wv_lo", [P, NT, NT, P], F32R)
        wpT = sb("wpT", [P, NT, C])
        pooled = sb("pooled", [P, 2, NT * PCH])
        m_hi = sb("m_hi", [P, 2, NT, C], F32R)
        m_lo = sb("m_lo", [P, 2, NT, C], F32R)
        g_hi = sb("g_hi", [P, NT, CG], F32R)
        g_lo = sb("g_lo", [P, NT, CG], F32R)
        xT_hi = sb("xT_hi", [P, 2, CG], F32R)
        xT_lo = sb("xT_lo", [P, 2, CG], F32R)
        t_hi = sb("t_hi", [P, 2, NT, KQ + 4], F32R)
        t_lo = sb("t_lo", [P, 2, NT, KQ + 4], F32R)
        work = sb("work", [P, 3 * C])
        ident = sb("ident", [P, P])
        own_head = sb("own_head", [P, P])
        group_avg = sb("group_avg", [P, P])
        squares = sb("squares", [P, NT * CH], mybir.dt.bfloat16)
        small = sb("small", [P, 100])

        st = work[:, 0:C].rearrange("p (b e) -> p b e", b=NT)
        key_rows = work[:, C:3 * C].rearrange("p (v b e) -> p v b e", v=2, b=NT)
        query_rows = work[:, C:2 * C].rearrange("p (b e) -> p b e", b=NT)
        logits = work[:, 2 * C:3 * C].rearrange("p (b e) -> p b e", b=NT)
        attn = work[:, 0:C].rearrange("p (b e) -> p b e", b=NT)
        p1_bv = work[:, 2 * C:3 * C]
        m_full = work[:, :].rearrange("p (t o) -> p t o", t=NT)

        cursor = [0]

        def cols(n):
            a = cursor[0]
            cursor[0] += n
            return small[:, a:a + n]

        neg_shift = cols(2)
        chunk_sum = cols(1)
        sum_squares = cols(NCH)
        all_squares = cols(1)
        two_sums = cols(1)
        all_sums = cols(1)
        mv = cols(2)
        gmv = cols(2)
        mean2 = cols(1)
        var = cols(1)
        rstd = cols(1)
        half_rstd = cols(1)
        negmean = cols(2)
        delta = cols(1)
        newton_a = cols(6)
        w_sums = cols(12)
        norm2 = cols(6)
        eff_bias = cols(6)
        n_eff_bias = cols(6)
        norm_b = cols(6)
        rnorm = cols(6)
        key_cols = cols(6)
        sum_q = cols(3)
        rq_temp = cols(3)
        neg_max = cols(3)
        exp_sum = cols(3)
        ones_col = xT_hi[:, 0, C:C + 1].bitcast(F32)
        kq_bias = small[:, 94:100].rearrange("p (s b) -> p s b", s=2)
        kq_bias_flat = small[:, 94:100]
        assert cursor[0] <= 94
        small2 = sb("small2", [P, 15])
        temp = small2[:, 0:3]
        bp = small2[:, 3:6]
        bv = small2[:, 6:9]
        bias = small2[:, 9:15]

        main_bank = [ctx.enter_context(nc.psum_tensor(f"main{i}", [P, CH], F32)) for i in range(3)]
        gram_a, gram_b, bank_c, bank_d, bank_f = [
            ctx.enter_context(nc.psum_tensor(n, [P, CH], F32))
            for n in ("gram_a", "gram_b", "bank_c", "bank_d", "bank_f")]

        s_bank = (bank_f, bank_f, bank_d)
        p1_bank = (bank_f, bank_c, bank_d)
        m_bank = (bank_c, bank_d, bank_f)

        raw_loaded = sem("raw_loaded")
        small_loaded = sem("small_loaded")
        x_loaded = [sem(f"x_loaded{s}") for s in range(XSLOTS)]
        out_stored = [sem(f"out_stored{s}") for s in range(2)]
        consts_step = sem("consts_step")
        consts_ready = sem("consts_ready")
        columns_ready = sem("columns_ready")
        w_transposed = sem("w_transposed")
        w_hi_ready = sem("w_hi_ready")
        w_lo_ready = sem("w_lo_ready")
        hi_ready = sem("hi_ready")
        lo_ready = sem("lo_ready")
        unit_done = sem("unit_done")
        evacuated = sem("evacuated")
        vec_step = sem("vec_step")
        pool_taken = sem("pool_taken")
        chunk_sum_ready = sem("chunk_sum_ready")
        shift_done = sem("shift_done")
        shift_ready = sem("shift_ready")
        centred = sem("centred")
        squares_taken = sem("squares_taken")
        turned = sem("turned")
        xT_hi_ready = sem("xT_hi_ready")
        xT_lo_ready = sem("xT_lo_ready")
        gram_done = sem("gram_done")
        sums_read = sem("sums_read")
        stats_ready = sem("stats_ready")
        group_done = sem("group_done")
        mean_ready = sem("mean_ready")
        g_hi_ready = sem("g_hi_ready")
        g_lo_ready = sem("g_lo_ready")
        t_cols_hi = sem("t_cols_hi")
        t_cols_lo = sem("t_cols_lo")
        t_done = sem("t_done")
        t_hi_ready = sem("t_hi_ready")
        t_lo_ready = sem("t_lo_ready")
        s_done = sem("s_done")
        s_read = sem("s_read")
        s_scaled = sem("s_scaled")
        s_turned = sem("s_turned")
        query_rows_ready = sem("query_rows_ready")
        logits_ready = sem("logits_ready")
        exp_done = sem("exp_done")
        attn_ready = sem("attn_ready")
        p1_done = sem("p1_done")
        p1_hi_ready = sem("p1_hi_ready")
        p1_lo_ready = sem("p1_lo_ready")
        m_done = sem("m_done")
        m_scaled = sem("m_scaled")
        m_full_ready = sem("m_full_ready")
        m_hi_ready = sem("m_hi_ready")
        m_ready = sem("m_ready")
        bias_done = sem("bias_done")
        bias_ready = sem("bias_ready")

        def wait_count(eng, semaphore, value):
            if isinstance(value, int) and value <= 0:
                return
            eng.wait_ge(semaphore, value)

        class Step:

            def __init__(self, b, parity, half):
                self.b, self.parity, self.half = b, parity, half

        def fixed(b):
            return Step(b, b % 2, b // 2)

        def following(s, n):
            return Step(s.b + n, (s.parity + n) % 2, s.half + (s.parity + n) // 2)

        def pair(i):
            return Step(2 * i + 1, 1, i), Step(2 * i + 2, 0, i + 1)

        def slot(s, j):
            return NCH * s.parity + j

        def gram_parts(g):
            gram_c = gram_b[:, CG - P:2 * CG - 3 * P]
            return ((g[:, 0, 0:P], gram_a[:, 0:P], half_rstd), (g[:, 0, P:CG], gram_a[:, P:CG], rstd),
                    (g[:, 1, P:2 * P], gram_b[:, 0:P], half_rstd), (g[:, 1, 2 * P:CG], gram_b[:, P:CG - P], rstd),
                    (g[:, 2, 2 * P:C], gram_c[:, 0:P], half_rstd), (g[:, 2, C:CG], gram_c[:, P:CG - 2 * P], rstd))

        raw = xs[:, XSLOTS - 3:XSLOTS, :].rearrange("p s n -> p (s n)")
        raw_qk = raw[:, 0:2 * NT * C].rearrange("p (k c) -> p k c", c=C)
        raw_v = raw[:, 2 * NT * C:3 * NT * C].rearrange("p (k c) -> p k c", c=C)
        raw_p = raw[:, 3 * NT * C:4 * NT * C].rearrange("p (t d) -> p t d", d=C)
        SMALL_LOADS = 4 + 2 + 1 + 1

        WEIGHTS_AFTER = 2

        block = ctx.enter_context(nc.Block())

        @block.sync
        def _(sp):
            def load(s, j):
                sp.dma_start(xs[:, slot(s, j), :].rearrange("p (t n) -> p t n", t=NT),
                             xv[bass.ds(s.b, 1), :, :, j * CH:(j + 1) * CH].rearrange(
                                 "a p t n -> p (a t) n")).then_inc(x_loaded[slot(s, j)], 16)

            def store(s, j):
                sp.wait_ge(evacuated, UNITS * s.b + NT * (j + 1))
                sp.dma_start(ov[bass.ds(s.b, 1), :, :, j * CH:(j + 1) * CH].rearrange(
                    "a p t n -> p (a t) n"), staged[:, j % 2, :, :]).then_inc(out_stored[j % 2], 16)

            def reload(s, j):
                n = following(s, (j + 1) // NCH)
                sp.wait_ge(lo_ready, NCH * s.b + j + 2)
                load(following(n, 2), (j + 1) % NCH)

            def step(s, reloads):
                for j in range(NCH):
                    if j < reloads:
                        reload(s, j)
                    store(s, j)

            for j in range(NCH):
                load(fixed(0), j)
            with nc.allow_non_contiguous_dma(reason="a few hundred single words, once"):
                for hh in range(4):
                    sp.dma_start(temp[HEAD * hh:HEAD * (hh + 1), :],
                                 temperature.rearrange("(b h) x y -> h (b x y)", h=4)[hh:hh + 1, :]
                                 .to_broadcast([HEAD, NT])).then_inc(small_loaded, 16)
                for k in range(2):
                    sp.dma_start(kq_bias[:, 1 - k, :], qk_b[k * C:(k + 1) * C].rearrange("(b p) -> p b", p=P))\
                        .then_inc(small_loaded, 16)
                sp.dma_start(bv, v_b.rearrange("(b p) -> p b", p=P)).then_inc(small_loaded, 16)
                sp.dma_start(bp, proj_b.rearrange("(p t) -> p t", t=NT)).then_inc(small_loaded, 16)
            for j in range(NCH - 3):
                load(fixed(1), j)
            sp.wait_ge(w_lo_ready, NT * NT + NT)
            sp.wait_ge(w_hi_ready, NT * NT + 2 * NT)
            for j in range(NCH - 3, NCH):
                load(fixed(1), j)
            sp.wait_ge(lo_ready, 1)
            load(fixed(2), 0)
            step(fixed(0), NCH)
            with sp.Fori(0, (B - 4) // 2) as i:
                for s in pair(i):
                    step(s, NCH)
            step(fixed(B - 3), NCH - 1)
            step(fixed(B - 2), 0)
            step(fixed(B - 1), 0)
            for s in range(2):
                sp.wait_ge(out_stored[s], 16 * B * NCH // 2)

        @block.gpsimd
        def _(pool):
            nc.gpsimd.memset(ident[:, :], 0.0).then_inc(consts_step, 1)
            nc.gpsimd.memset(own_head[:, :], 0.0).then_inc(consts_step, 1)
            nc.gpsimd.memset(group_avg[:, :], 1.0 / GP).then_inc(consts_step, 1)
            pool.wait_ge(consts_step, 3)
            nc.gpsimd.affine_select(out=ident[:, :], in_=ident[:, :], compare_op=ALU.not_equal, fill=1.0,
                                    base=0, pattern=[[-1, P]], channel_multiplier=1).then_inc(consts_ready, 1)
            for m, width, fill in ((own_head, HEAD, MASKED), (group_avg, GP, 0.0)):
                v = m[:, :].rearrange("p (k w) -> p k w", w=width)
                nc.gpsimd.affine_select(out=v, in_=v, compare_op=ALU.is_ge, fill=fill, base=0,
                                        pattern=[[-width, P // width], [0, width]],
                                        channel_multiplier=1).then_inc(consts_step, 1)
            pool.wait_ge(consts_step, 5)
            for m, width, fill in ((own_head, HEAD, MASKED), (group_avg, GP, 0.0)):
                v = m[:, :].rearrange("p (k w) -> p k w", w=width)
                nc.gpsimd.affine_select(out=v, in_=v, compare_op=ALU.is_ge, fill=fill, base=width - 1,
                                        pattern=[[width, P // width], [0, width]],
                                        channel_multiplier=-1).then_inc(consts_ready, 1)

        @block.tensor
        def _(pe):
            def three_passes(dst, lhs, rhs, start, stop, skip=False):
                nc.tensor.matmul(dst, lhs[0], rhs[0], start=start, stop=False, skip_group_check=skip)
                nc.tensor.matmul(dst, lhs[0], rhs[1], start=False, stop=False, skip_group_check=skip)
                return nc.tensor.matmul(dst, lhs[1], rhs[0], start=False, stop=stop, skip_group_check=skip)

            def unit(s, u):
                j, o = divmod(u, NT)
                if u == 0:
                    pe.wait_ge(m_ready, NT * (s.b + 1))
                if o == 0:
                    pe.wait_ge(lo_ready, NCH * s.b + j + 1)
                wait_count(pe, evacuated, UNITS * s.b + u - 2)
                for t in range(NT):
                    last = three_passes(
                        main_bank[u % 3][:, :],
                        (m_hi[:, s.parity, t, o * P:(o + 1) * P], m_lo[:, s.parity, t, o * P:(o + 1) * P]),
                        (x_hi[:, j % 2, t, :], x_lo[:, j % 2, t, :]), t == 0, t == NT - 1)
                last.then_inc(unit_done, 1)

            def shift(s):
                pe.wait_ge(chunk_sum_ready, s.b + 1)
                wait_count(pe, xT_lo_ready, NCH * s.b)
                nc.tensor.matmul(bank_f[:, 0:1], group_avg[:, :], chunk_sum, start=True, stop=True)\
                    .then_inc(shift_done, 1)

            def turn(s, j):
                pe.wait_ge(centred, NCH * s.b + j + 1)
                n = s.b - 1
                if j == 3:
                    wait_count(pe, s_read, NT * n + 2)
                if j == 5:
                    wait_count(pe, query_rows_ready, n + 1)
                if j == 6:
                    wait_count(pe, p1_lo_ready, NT * n + 1)
                if j == 7:
                    wait_count(pe, m_scaled, NT * n + 3)
                wait_count(pe, xT_lo_ready, NCH * s.b + j)
                for t in range(NT):
                    last = nc.tensor.transpose(bank_f[:, t * P:(t + 1) * P],
                                               pooled[:, j % 2, t * PCH:(t + 1) * PCH], ident[:, :])
                last.then_inc(turned, 1)

            def gram(s, c):
                pe.wait_ge(xT_lo_ready, NCH * s.b + c + 1)
                if c == 0:
                    wait_count(pe, g_lo_ready, s.b)
                h, l = xT_hi[:, c % 2, :], xT_lo[:, c % 2, :]
                first, final = c == 0, c == NCH - 1
                three_passes(gram_a[:, 0:CG], (h[:, 0:P], l[:, 0:P]), (h[:, 0:CG], l[:, 0:CG]), first, final)
                three_passes(gram_b[:, 0:CG - P], (h[:, P:2 * P], l[:, P:2 * P]),
                             (h[:, P:CG], l[:, P:CG]), first, final, skip=True)
                three_passes(gram_b[:, CG - P:2 * CG - 3 * P], (h[:, 2 * P:3 * P], l[:, 2 * P:3 * P]),
                             (h[:, 2 * P:CG], l[:, 2 * P:CG]), False, final, skip=True)\
                    .then_inc(gram_done, 1)

            def intake(s, u):
                if u == SHIFT_AT:
                    shift(s)
                if u in GRAM_AT:
                    gram(s, GRAM_AT[u])
                if u in TURN_AT:
                    turn(s, TURN_AT[u])

            def group_stats(s):
                pe.wait_ge(stats_ready, s.b + 1)
                wait_count(pe, bias_ready, s.b)
                nc.tensor.matmul(bank_c[:, 0:2], group_avg[:, :], mv, start=True, stop=True)\
                    .then_inc(group_done, 1)

            def t_block(s, blk):
                if blk == 0:
                    pe.wait_ge(g_lo_ready, s.b + 1)
                    wait_count(pe, m_scaled, NT * s.b)
                else:
                    pe.wait_ge(t_lo_ready, NT * s.b + blk)
                for i, dst in enumerate((bank_c[:, 0:KQ], bank_c[:, KQ:2 * KQ], bank_d[:, 0:KQ])):
                    for k in range(i + 1):
                        last = three_passes(dst, (g_hi[:, k, i * P:(i + 1) * P], g_lo[:, k, i * P:(i + 1) * P]),
                                            (wT_hi[:, k, blk, :], wT_lo[:, k, blk, :]), k == 0, k == i)
                last.then_inc(t_done, 1)

            def s_block(s, blk, turns):
                pe.wait_ge(t_lo_ready, NT * s.b + blk + 1)
                if blk == 0:
                    pe.wait_ge(t_cols_lo, s.b + 1)
                wait_count(pe, s_read, NT * s.b + blk)
                if blk == 2:
                    pe.wait_ge(t_lo_ready, NT * (s.b + 1))
                elif turns is not None:
                    pe.wait_ge(xT_lo_ready, turns)
                buf = blk % 2
                bank = s_bank[blk]
                for k in range(NT):
                    three_passes(bank[:, 0:KQ + 4], (wT_hi[:, k, blk, 0:P], wT_lo[:, k, blk, 0:P]),
                                 (t_hi[:, buf, k, 0:KQ + 4], t_lo[:, buf, k, 0:KQ + 4]), k == 0, False, skip=True)
                for k in range(NT):
                    three_passes(bank[:, P:KQ], (t_hi[:, buf, k, 0:P], t_lo[:, buf, k, 0:P]),
                                 (wT_hi[:, k, blk, P:KQ], wT_lo[:, k, blk, P:KQ]), False, k == NT - 1, skip=True)
                for k in range(NT):
                    last = three_passes(bank[:, KQ + 4:KQ + 8 + P],
                                        (wT_hi[:, k, blk, P:KQ], wT_lo[:, k, blk, P:KQ]),
                                        (t_hi[:, buf, k, P:KQ + 4], t_lo[:, buf, k, P:KQ + 4]),
                                        k == 0, k == NT - 1)
                last.then_inc(s_done, 1)

            def turn_scores(s, turns):
                pe.wait_ge(s_scaled, s.b + 1)
                for src, bank in ((st, bank_c), (key_rows[:, 0, :, :], bank_d), (key_rows[:, 1, :, :], bank_f)):
                    if bank is bank_f and turns is not None:
                        pe.wait_ge(xT_lo_ready, turns)
                    for blk in range(NT):
                        last = nc.tensor.transpose(bank[:, blk * P:(blk + 1) * P], src[:, blk, :], ident[:, :])
                last.then_inc(s_turned, 1)

            def fold_proj(s, turns):
                pe.wait_ge(attn_ready, s.b + 1)
                for blk, bank in enumerate(p1_bank):
                    if bank is bank_f and turns is not None:
                        pe.wait_ge(xT_lo_ready, turns)
                    nc.tensor.matmul(bank[:, 0:C], attn[:, blk, :], wpT[:, blk, :], start=True, stop=True)\
                        .then_inc(p1_done, 1)

            def fold_value(s, turns):
                pe.wait_ge(p1_lo_ready, NT * (s.b + 1))
                for o in range(NT):
                    last = nc.tensor.matmul(bank_c[:, C + o:C + o + 1], p1_bv[:, o * P:(o + 1) * P],
                                            ones_col, start=True, stop=True)
                last.then_inc(bias_done, 1)
                for t, bank in enumerate(m_bank):
                    if bank is bank_f and turns is not None:
                        pe.wait_ge(xT_lo_ready, turns)
                    for blk in range(NT):
                        last = three_passes(bank[:, 0:C], (wv_hi[:, blk, t, :], wv_lo[:, blk, t, :]),
                                            (g_hi[:, blk, 0:C], g_lo[:, blk, 0:C]), blk == 0, blk == NT - 1)
                    last.then_inc(m_done, 1)

            def chain(s, u, with_intake=True):
                def turns(u):
                    return NCH * (s.b + 1) + sum(v <= u for v in TURN_AT) if with_intake else None

                if u == GROUP_AT:
                    group_stats(s)
                if u in T_AT:
                    t_block(s, T_AT[u])
                if u in S_AT:
                    s_block(s, S_AT[u], turns(u))
                if u == LOGITS_AT:
                    turn_scores(s, turns(LOGITS_AT))
                if u == PROJ_AT:
                    fold_proj(s, turns(PROJ_AT))
                if u == VALUE_AT:
                    fold_value(s, turns(VALUE_AT))

            def weights():
                pe.wait_ge(raw_loaded, 16 * 3)
                for n in range(NT * NT):
                    blk, t = divmod(n, NT)
                    if n >= 3:
                        pe.wait_ge(w_lo_ready, n - 2)
                    for half, row in ((0, NT + blk), (1, blk)):
                        last = nc.tensor.transpose(main_bank[n % 3][:, half * P:(half + 1) * P],
                                                   raw_qk[:, row, :].rearrange("p (c t) -> p t c", t=NT)[:, t, :],
                                                   ident[:, :])
                    last.then_inc(w_transposed, 1)
                for blk in range(NT):
                    for t in range(NT):
                        last = nc.tensor.transpose((bank_c, bank_d)[blk % 2][:, t * P:(t + 1) * P],
                                                   raw_p[:, t, blk * P:(blk + 1) * P], ident[:, :])
                    last.then_inc(w_transposed, 1)
                    if blk == 0:
                        pe.wait_ge(w_lo_ready, NT * NT)
                    pe.wait_ge(w_hi_ready, NT * NT + blk)

            pe.wait_ge(consts_ready, 3)
            pe.wait_ge(columns_ready, 2)
            for j in range(NCH):
                if j == 0:
                    shift(fixed(0))
                if j == WEIGHTS_AFTER:
                    weights()
                turn(fixed(0), j)
                if j >= 1:
                    gram(fixed(0), j - 1)
            gram(fixed(0), NCH - 1)
            pe.wait_ge(w_hi_ready, NT * NT + NT)
            for u in range(UNITS):
                intake(fixed(1), u)
                chain(fixed(0), u)

            def step(s, with_chain=True, with_intake=True):
                for u in range(UNITS):
                    if with_intake:
                        intake(following(s, 2), u)
                    if with_chain:
                        chain(following(s, 1), u, with_intake)
                    unit(s, u)

            step(fixed(0))
            with pe.Fori(0, (B - 4) // 2) as i:
                for s in pair(i):
                    step(s)
            step(fixed(B - 3))
            step(fixed(B - 2), with_intake=False)
            step(fixed(B - 1), with_chain=False, with_intake=False)

        @block.scalar
        def _(act):
            def split_hi(s, j):
                act.wait_ge(x_loaded[slot(s, j)], 16 * (s.half + 1))
                if j < 2:
                    act.wait_ge(mean_ready, s.b + 1)
                wait_count(act, unit_done, UNITS * s.b + NT * (j - 1))
                nc.scalar.activation(x_hi[:, j % 2, :, :].rearrange("p t n -> p (t n)"), xs[:, slot(s, j), :],
                                     ACT.Identity, bias=negmean[:, s.parity:s.parity + 1]).then_inc(hi_ready, 1)

            def evacuate(s, u):
                j, o = divmod(u, NT)
                if u == 0:
                    act.wait_ge(bias_ready, s.b + 1)
                if o == 0:
                    wait_count(act, out_stored[j % 2], 16 * ((NCH // 2) * s.b + j // 2))
                act.wait_ge(unit_done, UNITS * s.b + u + 1)
                nc.scalar.activation(staged[:, j % 2, o, :], main_bank[u % 3][:, :], ACT.Identity,
                                     bias=bias[:, NT * s.parity + o:NT * s.parity + o + 1]).then_inc(evacuated, 1)

            def take_squares(s, j):
                act.wait_ge(x_loaded[slot(s, j)], 16 * (s.half + 1))
                if j == 0:
                    act.wait_ge(shift_ready, s.b + 1)
                    wait_count(act, stats_ready, s.b)
                wait_count(act, squares_taken, NCH * s.b + j)
                nc.scalar.activation(squares[:, :], xs[:, slot(s, j), :], ACT.Square,
                                     bias=neg_shift[:, s.parity:s.parity + 1],
                                     accum_out=sum_squares[:, j:j + 1]).then_inc(squares_taken, 1)

            def xT_high(s, j):
                act.wait_ge(turned, NCH * s.b + j + 1)
                wait_count(act, gram_done, NCH * s.b + j - 1)
                nc.scalar.activation(xT_hi[:, j % 2, 0:C], bank_f[:, 0:C], ACT.Copy).then_inc(xT_hi_ready, 1)

            def intake(s, u):
                if u in TURN_AT:
                    xT_high(s, TURN_AT[u])

            def gram_high(s):
                act.wait_ge(mean_ready, s.b + 1)
                for dst, src, scale in gram_parts(g_hi):
                    last = nc.scalar.activation(dst, src, ACT.Copy, scale=scale)
                last.then_inc(g_hi_ready, 1)
                act.wait_ge(g_hi_ready, s.b + 1)
                wait_count(act, s_done, NT * s.b)
                for buf in range(2):
                    nc.scalar.activation(t_hi[:, buf, :, KQ:KQ + 2], g_hi[:, :, C:CG].bitcast(F32), ACT.Copy)
                    last = nc.scalar.activation(t_hi[:, buf, :, KQ + 2:KQ + 4],
                                                delta.unsqueeze(2).to_broadcast([P, NT, 2]), ACT.Copy)
                last.then_inc(t_cols_hi, 1)

            def t_high(s, blk):
                act.wait_ge(t_done, NT * s.b + blk + 1)
                if blk == 2:
                    act.wait_ge(s_done, NT * s.b + 1)
                nc.scalar.activation(t_hi[:, blk % 2, 0:2, 0:KQ], bank_c[:, :].rearrange("p (i c) -> p i c", i=2),
                                     ACT.Copy, scale=rstd)
                nc.scalar.activation(t_hi[:, blk % 2, 2, 0:KQ], bank_d[:, 0:KQ], ACT.Copy, scale=rstd)\
                    .then_inc(t_hi_ready, 1)

            def scale_query_rows(s):
                act.wait_ge(s_turned, s.b + 1)
                for blk in range(NT):
                    last = nc.scalar.activation(query_rows[:, blk, :], bank_f[:, blk * P:(blk + 1) * P], ACT.Copy,
                                                scale=eff_bias[:, NT + blk:NT + blk + 1])
                last.then_inc(query_rows_ready, 1)

            def exps(s):
                act.wait_ge(logits_ready, s.b + 1)
                for blk in range(NT):
                    last = nc.scalar.activation(attn[:, blk, :], logits[:, blk, :], ACT.Exp,
                                                bias=neg_max[:, blk:blk + 1], accum_out=exp_sum[:, blk:blk + 1])
                last.then_inc(exp_done, 1)

            def p1_high(s):
                for blk, bank in enumerate(p1_bank):
                    act.wait_ge(p1_done, NT * s.b + blk + 1)
                    nc.scalar.activation(g_hi[:, blk, 0:C], bank[:, 0:C], ACT.Copy).then_inc(p1_hi_ready, 1)

            def scale_m(s):
                for t, bank in enumerate(m_bank):
                    act.wait_ge(m_done, NT * s.b + t + 1)
                    nc.scalar.activation(m_full[:, t, :], bank[:, 0:C], ACT.Copy, scale=rstd).then_inc(m_scaled, 1)

            def m_high(s):
                for t in range(NT):
                    act.wait_ge(m_full_ready, NT * s.b + t + 1)
                    nc.scalar.activation(m_hi[:, s.parity, t, :], m_full[:, t, :], ACT.Copy).then_inc(m_hi_ready, 1)

            def chain(s, u):
                if u == SPLIT_GRAM_AT:
                    gram_high(s)
                if u in T_AT:
                    t_high(s, T_AT[u])
                if u == LOGITS_AT:
                    scale_query_rows(s)
                if u == SOFTMAX_AT:
                    exps(s)
                if u == PROJ_AT:
                    p1_high(s)
                if u == VALUE_AT:
                    scale_m(s)
                    m_high(s)

            act.dma_start(raw_qk, qk_w.rearrange("(k p) c -> p k c", p=P)).then_inc(raw_loaded, 16)
            act.dma_start(raw_v, v_w.rearrange("(k p) c -> p k c", p=P)).then_inc(raw_loaded, 16)
            act.dma_start(raw_p, proj_w.rearrange("(p t) d -> p t d", t=NT)).then_inc(raw_loaded, 16)

            def weights():
                for n in range(NT * NT):
                    blk, t = divmod(n, NT)
                    act.wait_ge(w_transposed, n + 1)
                    nc.scalar.activation(wT_hi[:, t, blk, :], main_bank[n % 3][:, 0:KQ], ACT.Copy)\
                        .then_inc(w_hi_ready, 1)
                for blk in range(NT):
                    act.wait_ge(w_transposed, NT * NT + blk + 1)
                    nc.scalar.activation(wpT[:, blk, :], (bank_c, bank_d)[blk % 2][:, 0:C], ACT.Copy)\
                        .then_inc(w_hi_ready, 1)
                for blk in range(NT):
                    nc.scalar.activation(wv_hi[:, blk, :, :], raw_v[:, blk, :].rearrange("p (c t) -> p t c", t=NT),
                                         ACT.Copy).then_inc(w_hi_ready, 1)

            for j in range(NCH):
                if j == WEIGHTS_AFTER:
                    weights()
                xT_high(fixed(0), j)
                take_squares(fixed(0), j)
            act.wait_ge(small_loaded, 16 * SMALL_LOADS)
            for u in range(UNITS):
                intake(fixed(1), u)
                chain(fixed(0), u)
                if u in FIRST_SPLIT_AT:
                    split_hi(fixed(0), FIRST_SPLIT_AT[u])
                if u in SQUARES_AT:
                    take_squares(fixed(1), SQUARES_AT[u])

            def step(s, with_chain=True, with_intake=True):
                for u in range(UNITS):
                    if with_intake:
                        intake(following(s, 2), u)
                    if with_chain:
                        chain(following(s, 1), u)
                    evacuate(s, u)
                    j, o = divmod(u, NT)
                    if o == NT - 1:
                        if j + 2 < NCH:
                            split_hi(s, j + 2)
                        elif with_chain:
                            split_hi(following(s, 1), j + 2 - NCH)
                    if with_intake and u in SQUARES_AT:
                        take_squares(following(s, 2), SQUARES_AT[u])

            step(fixed(0))
            with act.Fori(0, (B - 4) // 2) as i:
                for s in pair(i):
                    step(s)
            step(fixed(B - 3))
            step(fixed(B - 2), with_intake=False)
            step(fixed(B - 1), with_chain=False, with_intake=False)

        @block.vector
        def _(dve):
            links = {"base": 0, "count": 0, "setup": 0, "per_image": None}

            def link(ins):
                links["count"] += 1
                ins.then_inc(vec_step, 1)
                dve.wait_ge(vec_step, links["base"] + links["count"])

            def open_links(s, count=0):
                links["count"] = count
                links["base"] = links["setup"] + (0 if links["per_image"] is None else links["per_image"] * s.b)

            def close_links():
                assert links["per_image"] in (None, links["count"])
                links["per_image"] = links["count"]

            def rsqrt(y, v):
                a = newton_a[:, 0:v.shape[1]]
                link(nc.vector.tensor_scalar(a.bitcast(I32), v.bitcast(I32), 1, None, ALU.logical_shift_right))
                link(nc.vector.tensor_scalar(y.bitcast(I32), a.bitcast(I32), -1.0, RSQRT_MAGIC, ALU.mult, ALU.add))
                for _ in range(3):
                    link(nc.vector.scalar_tensor_tensor(out=a, in0=y, scalar=-0.5, in1=v,
                                                        op0=ALU.mult, op1=ALU.mult))
                    link(nc.vector.tensor_tensor(a, a, y, ALU.mult))
                    link(nc.vector.scalar_tensor_tensor(out=y, in0=a, scalar=1.5, in1=y,
                                                        op0=ALU.add, op1=ALU.mult))

            def split_lo(s, j):
                dve.wait_ge(hi_ready, NCH * s.b + j + 1)
                nc.vector.scalar_tensor_tensor(
                    out=x_lo[:, j % 2, :, :].rearrange("p t n -> p (t n)"), in0=xs[:, slot(s, j), :],
                    scalar=negmean[:, s.parity:s.parity + 1],
                    in1=x_hi[:, j % 2, :, :].rearrange("p t n -> p (t n)").bitcast(F32),
                    op0=ALU.add, op1=ALU.subtract).then_inc(lo_ready, 1)

            def take_pool(s, j):
                dst = pooled[:, j % 2, :]
                dve.wait_ge(x_loaded[slot(s, j)], 16 * (s.half + 1))
                wait_count(dve, turned, NCH * s.b + j - 1)
                quads = xs[:, slot(s, j), :].rearrange("p (r a c w) -> p r c a w", a=POOL, w=POOL, c=W // POOL)
                nc.vector.tensor_reduce(dst, quads, AX.XY, ALU.add).then_inc(pool_taken, 1)
                dve.wait_ge(pool_taken, NCH * s.b + j + 1)
                if j == 0:
                    nc.vector.tensor_reduce(chunk_sum, dst, AX.X, ALU.add).then_inc(chunk_sum_ready, 1)
                else:
                    centre(s, j)

            def take_shift(s):
                dve.wait_ge(shift_done, s.b + 1)
                nc.vector.tensor_scalar(neg_shift[:, s.parity:s.parity + 1], bank_f[:, 0:1], -1.0 / (NT * CH), None,
                                        ALU.mult).then_inc(shift_ready, 1)
                dve.wait_ge(shift_ready, s.b + 1)
                centre(s, 0)

            def centre(s, j):
                dst = pooled[:, j % 2, :]
                nc.vector.tensor_scalar(dst, dst, 1.0 / (POOL * POOL), neg_shift[:, s.parity:s.parity + 1],
                                        ALU.mult, ALU.add).then_inc(centred, 1)

            def xT_low(s, j):
                dve.wait_ge(xT_hi_ready, NCH * s.b + j + 1)
                nc.vector.tensor_tensor(xT_lo[:, j % 2, 0:C], bank_f[:, 0:C], xT_hi[:, j % 2, 0:C].bitcast(F32),
                                        ALU.subtract).then_inc(xT_lo_ready, 1)

            def intake(s, u):
                if u == SHIFT_AT - 1:
                    take_shift(s)
                if u in TURN_AT:
                    xT_low(s, TURN_AT[u])
                if u == UNITS - 1:
                    open_links(s)
                    partition_stats(s)

            def partition_stats(s):
                dve.wait_ge(gram_done, NCH * (s.b + 1))
                link(nc.vector.tensor_reduce(two_sums, gram_b[:, KQ:KQ + P + 3:P + 2], AX.X, ALU.add))
                nc.vector.scalar_tensor_tensor(out=all_sums, in0=gram_a[:, C:C + 1], scalar=1.0, in1=two_sums,
                                               op0=ALU.mult, op1=ALU.add).then_inc(sums_read, 1)
                dve.wait_ge(squares_taken, NCH * (s.b + 1))
                link(nc.vector.tensor_reduce(all_squares, sum_squares, AX.X, ALU.add))
                dve.wait_ge(sums_read, s.b + 1)
                link(nc.vector.tensor_scalar(mv[:, 0:1], all_sums, 1.0 / (NT * NPOS), None, ALU.mult))
                nc.vector.tensor_scalar(mv[:, 1:2], all_squares, 1.0 / (NT * HW), None, ALU.mult)\
                    .then_inc(stats_ready, 1)
                links["stats"] = links["count"]

            def group_scale(s):
                dve.wait_ge(group_done, s.b + 1)
                link(nc.vector.tensor_copy(gmv, bank_c[:, 0:2]))
                link(nc.vector.tensor_tensor(mean2, gmv[:, 0:1], gmv[:, 0:1], ALU.mult))
                link(nc.vector.scalar_tensor_tensor(out=var, in0=gmv[:, 1:2], scalar=GN_EPS, in1=mean2,
                                                    op0=ALU.add, op1=ALU.subtract))
                rsqrt(rstd, var)
                nc.vector.tensor_scalar(half_rstd, rstd, 0.5, None, ALU.mult)
                link(nc.vector.tensor_tensor(negmean[:, s.parity:s.parity + 1],
                                             neg_shift[:, s.parity:s.parity + 1], gmv[:, 0:1], ALU.subtract))
                nc.vector.tensor_tensor(delta, gmv[:, 0:1], rstd, ALU.mult).then_inc(mean_ready, 1)

            def gram_low(s):
                dve.wait_ge(g_hi_ready, s.b + 1)
                for (dst, src, scale), (high, _, _) in zip(gram_parts(g_lo), gram_parts(g_hi)):
                    last = nc.vector.scalar_tensor_tensor(out=dst, in0=src, scalar=scale, in1=high.bitcast(F32),
                                                          op0=ALU.mult, op1=ALU.subtract)
                last.then_inc(g_lo_ready, 1)
                dve.wait_ge(g_lo_ready, s.b + 1)
                dve.wait_ge(t_cols_hi, s.b + 1)
                dve.wait_ge(mean_ready, s.b + 1)
                for buf in range(2):
                    nc.vector.tensor_copy(t_lo[:, buf, :, KQ:KQ + 2], g_lo[:, :, C:CG])
                    last = nc.vector.tensor_tensor(t_lo[:, buf, :, KQ + 2:KQ + 4],
                                                   delta.unsqueeze(2).to_broadcast([P, NT, 2]),
                                                   t_hi[:, buf, :, KQ + 2:KQ + 4].bitcast(F32), ALU.subtract)
                last.then_inc(t_cols_lo, 1)

            def t_low(s, blk):
                dve.wait_ge(t_hi_ready, NT * s.b + blk + 1)
                nc.vector.scalar_tensor_tensor(out=t_lo[:, blk % 2, 0:2, 0:KQ],
                                               in0=bank_c[:, :].rearrange("p (i c) -> p i c", i=2), scalar=rstd,
                                               in1=t_hi[:, blk % 2, 0:2, 0:KQ].bitcast(F32),
                                               op0=ALU.mult, op1=ALU.subtract)
                nc.vector.scalar_tensor_tensor(out=t_lo[:, blk % 2, 2, 0:KQ], in0=bank_d[:, 0:KQ], scalar=rstd,
                                               in1=t_hi[:, blk % 2, 2, 0:KQ].bitcast(F32),
                                               op0=ALU.mult, op1=ALU.subtract).then_inc(t_lo_ready, 1)

            def read_scores(s, blk):
                dve.wait_ge(s_done, NT * s.b + blk + 1)
                bank = s_bank[blk]
                ws = w_sums.rearrange("p (v s b) -> p v s b", v=2, s=2)
                nc.vector.tensor_copy(ws[:, :, 0, blk], bank[:, KQ:KQ + 4:2])
                nc.vector.tensor_copy(ws[:, :, 1, blk], bank[:, KQ + 4 + P:KQ + 8 + P:2])
                nc.vector.tensor_copy(st[:, blk, :], bank[:, P:2 * P])
                nc.vector.scalar_tensor_tensor(out=key_rows[:, 0, blk, :], in0=bank[:, 0:P], scalar=2.0,
                                               in1=ident[:, :], op0=ALU.mult, op1=ALU.mult,
                                               accum_out=norm2[:, blk:blk + 1])
                nc.vector.scalar_tensor_tensor(out=key_rows[:, 1, blk, :], in0=bank[:, KQ + 4:KQ + 4 + P],
                                               scalar=2.0, in1=ident[:, :], op0=ALU.mult, op1=ALU.mult,
                                               accum_out=norm2[:, NT + blk:NT + blk + 1]).then_inc(s_read, 1)

            def scale_scores(s):
                dve.wait_ge(s_read, NT * (s.b + 1))
                w_s, w_delta = w_sums[:, 0:2 * NT], w_sums[:, 2 * NT:4 * NT]
                link(nc.vector.tensor_tensor(eff_bias, kq_bias_flat, w_delta, ALU.subtract))
                link(nc.vector.tensor_scalar(n_eff_bias, eff_bias, float(NPOS), None, ALU.mult))
                link(nc.vector.scalar_tensor_tensor(out=norm_b, in0=w_s, scalar=2.0, in1=n_eff_bias,
                                                    op0=ALU.mult, op1=ALU.add))
                link(nc.vector.tensor_tensor(norm_b, norm_b, eff_bias, ALU.mult))
                link(nc.vector.tensor_tensor(norm_b, norm_b, norm2, ALU.add))
                link(nc.vector.tensor_scalar(norm_b, norm_b, NORM_EPS * NORM_EPS, None, ALU.max))
                rsqrt(rnorm, norm_b)
                nc.vector.tensor_tensor(key_cols[:, 0:NT], rnorm[:, 0:NT], eff_bias[:, 0:NT], ALU.mult)
                link(nc.vector.tensor_tensor(key_cols[:, NT:2 * NT], rnorm[:, 0:NT], w_s[:, 0:NT], ALU.mult))
                nc.vector.tensor_tensor(sum_q, w_s[:, NT:2 * NT], n_eff_bias[:, NT:2 * NT], ALU.add)
                nc.vector.tensor_tensor(rq_temp, rnorm[:, NT:2 * NT], temp, ALU.mult)
                nc.vector.tensor_tensor(st, st, rnorm[:, 0:NT].unsqueeze(2).to_broadcast([P, NT, P]), ALU.mult)
                nc.vector.tensor_copy(work[:, C:3 * C].rearrange("p (k e) -> p k e", e=P),
                                      key_cols.unsqueeze(2).to_broadcast([P, 2 * NT, P])).then_inc(s_scaled, 1)

            def make_logits(s):
                dve.wait_ge(s_turned, s.b + 1)
                dve.wait_ge(s_scaled, s.b + 1)
                v = [bank[:, 0:C].rearrange("p (b e) -> p b e", b=NT) for bank in (bank_c, bank_d)]
                link(nc.vector.tensor_tensor(st, v[1], sum_q.unsqueeze(2).to_broadcast([P, NT, P]), ALU.mult))
                link(nc.vector.tensor_tensor(st, v[0], st, ALU.add))
                dve.wait_ge(query_rows_ready, s.b + 1)
                link(nc.vector.tensor_tensor(st, st, query_rows, ALU.add))
                for blk in range(NT):
                    last = nc.vector.scalar_tensor_tensor(out=logits[:, blk, :], in0=st[:, blk, :],
                                                          scalar=rq_temp[:, blk:blk + 1], in1=own_head[:, :],
                                                          op0=ALU.mult, op1=ALU.add)
                link(last)
                nc.vector.tensor_reduce(neg_max, logits, AX.X, ALU.max, negate=True).then_inc(logits_ready, 1)

            def normalise_attn(s):
                dve.wait_ge(exp_done, s.b + 1)
                link(nc.vector.reciprocal(exp_sum, exp_sum))
                nc.vector.tensor_tensor(attn, attn, exp_sum.unsqueeze(2).to_broadcast([P, NT, P]), ALU.mult)\
                    .then_inc(attn_ready, 1)

            def p1_low(s):
                for blk, bank in enumerate(p1_bank):
                    dve.wait_ge(p1_hi_ready, NT * s.b + blk + 1)
                    if blk == 0:
                        link(nc.vector.tensor_scalar(p1_bv, bank[:, 0:C], bv[:, 0:1], None, ALU.mult))
                    else:
                        link(nc.vector.scalar_tensor_tensor(out=p1_bv, in0=bank[:, 0:C], scalar=bv[:, blk:blk + 1],
                                                            in1=p1_bv, op0=ALU.mult, op1=ALU.add))
                    nc.vector.tensor_tensor(g_lo[:, blk, 0:C], bank[:, 0:C], g_hi[:, blk, 0:C].bitcast(F32),
                                            ALU.subtract).then_inc(p1_lo_ready, 1)

            def add_identity(s):
                for t in range(NT):
                    dve.wait_ge(m_scaled, NT * s.b + t + 1)
                    d = m_full[:, t, t * P:(t + 1) * P]
                    nc.vector.tensor_tensor(d, d, ident[:, :], ALU.add).then_inc(m_full_ready, 1)

            def m_low(s):
                for t in range(NT):
                    dve.wait_ge(m_hi_ready, NT * s.b + t + 1)
                    nc.vector.tensor_tensor(m_lo[:, s.parity, t, :], m_full[:, t, :],
                                            m_hi[:, s.parity, t, :].bitcast(F32), ALU.subtract).then_inc(m_ready, 1)

            def make_bias(s):
                dve.wait_ge(bias_done, s.b + 1)
                nc.vector.scalar_tensor_tensor(out=bias[:, NT * s.parity:NT * (s.parity + 1)], in0=bank_c[:, C:C + NT],
                                               scalar=negmean[:, s.parity:s.parity + 1], in1=bp,
                                               op0=ALU.subtract, op1=ALU.add)\
                    .then_inc(bias_ready, 1)

            def chain(s, u):
                if u == GROUP_AT:
                    open_links(s, links["stats"])
                    group_scale(s)
                if u == SPLIT_GRAM_AT:
                    gram_low(s)
                if u in T_AT:
                    t_low(s, T_AT[u])
                if u in S_AT:
                    read_scores(s, S_AT[u])
                    if S_AT[u] == NT - 1:
                        scale_scores(s)
                if u == LOGITS_AT:
                    make_logits(s)
                if u == SOFTMAX_AT:
                    normalise_attn(s)
                if u == PROJ_AT:
                    p1_low(s)
                if u == VALUE_AT:
                    add_identity(s)
                    m_low(s)
                    make_bias(s)
                    close_links()

            def weights():
                for n in range(NT * NT):
                    blk, t = divmod(n, NT)
                    dve.wait_ge(w_hi_ready, n + 1)
                    nc.vector.tensor_tensor(wT_lo[:, t, blk, :], main_bank[n % 3][:, 0:KQ],
                                            wT_hi[:, t, blk, :].bitcast(F32), ALU.subtract).then_inc(w_lo_ready, 1)
                for blk in range(NT):
                    dve.wait_ge(w_hi_ready, NT * NT + NT + blk + 1)
                    nc.vector.tensor_tensor(wv_lo[:, blk, :, :], raw_v[:, blk, :].rearrange("p (c t) -> p t c", t=NT),
                                            wv_hi[:, blk, :, :].bitcast(F32), ALU.subtract).then_inc(w_lo_ready, 1)

            nc.vector.memset(xT_hi[:, :, C:CG].bitcast(F32), 1.0).then_inc(columns_ready, 1)
            nc.vector.memset(xT_lo[:, :, C:CG].bitcast(F32), 0.0).then_inc(columns_ready, 1)
            take_pool(fixed(0), 0)
            take_shift(fixed(0))
            for j in range(NCH):
                if j == WEIGHTS_AFTER:
                    weights()
                if j + 1 < NCH:
                    take_pool(fixed(0), j + 1)
                xT_low(fixed(0), j)
            dve.wait_ge(consts_ready, 3)
            open_links(fixed(0))
            partition_stats(fixed(0))
            dve.wait_ge(small_loaded, 16 * SMALL_LOADS)
            for u in range(UNITS):
                intake(fixed(1), u)
                chain(fixed(0), u)
                if u in POOL_AT:
                    take_pool(fixed(1), POOL_AT[u])
                if u in FIRST_SPLIT_AT:
                    split_lo(fixed(0), FIRST_SPLIT_AT[u])

            def step(s, with_chain=True, with_intake=True):
                for u in range(UNITS):
                    j, o = divmod(u, NT)
                    if with_intake:
                        intake(following(s, 2), u)
                    if with_chain:
                        chain(following(s, 1), u)
                    if with_intake and u in POOL_AT:
                        take_pool(following(s, 2), POOL_AT[u])
                    if o == NT - 1:
                        if j + 2 < NCH:
                            split_lo(s, j + 2)
                        elif with_chain:
                            split_lo(following(s, 1), j + 2 - NCH)

            step(fixed(0))
            with dve.Fori(0, (B - 4) // 2) as i:
                for s in pair(i):
                    step(s)
            step(fixed(B - 3))
            step(fixed(B - 2), with_intake=False)
            step(fixed(B - 1), with_chain=False, with_intake=False)


_INS = ["x", "L0_conv_qk_w", "L0_conv_qk_b", "L0_conv_v_w", "L0_conv_v_b", "L0_conv_proj_w", "L0_conv_proj_b",
        "L0_conv_temperature"]


def kernel(**inputs):
    import numpy as np
    import concourse.bacc as bacc
    from concourse import mybir as mb
    from concourse.bass_utils import run_bass_kernel_spmd as run

    nc = bacc.Bacc("TRN2", target_bir_lowering=False, num_devices=1, dynamic_dma_scratch_size=256)
    arrays, args = {}, []
    for name in _INS:
        a = np.ascontiguousarray(inputs[name])
        arrays[name] = a
        args.append(nc.dram_tensor(name, a.shape, mb.dt.from_np(a.dtype), kind="ExternalInput").ap())
    y = nc.dram_tensor("y", inputs["x"].shape, mb.dt.float32, kind="ExternalOutput").ap()
    conv_attention_program(nc, *args, y)
    r = run(nc, [arrays], core_ids=[0])
    return r.results[0]["y"]
```
